# Optimizing a Trainium2 kernel written in Bass

```python
import numpy as np
import jax
import jax.numpy as jnp

def _softmax(x, axis=-1):
    return jax.nn.softmax(x, axis=axis)

def _gelu(x):
    return jax.nn.gelu(x, approximate=True)

def _silu(x):
    return jax.nn.silu(x)

def _sigmoid(x):
    return jax.nn.sigmoid(x)

def _layernorm(x, axis=-1, eps=1e-05):
    m = jnp.mean(x, axis=axis, keepdims=True)
    v = jnp.var(x, axis=axis, keepdims=True)
    return (x - m) / jnp.sqrt(v + eps)

def _scatter_add(tgt, idx, src, axis=0):
    return tgt.at[idx].add(src)

def _segment_sum(src, seg, n):
    return jax.ops.segment_sum(src, seg, n)
kernel_name = 'mk_prb_d1_jaxref_r4_f2e13b'

def setup_inputs(seed: int=0):
    np.random.seed(seed)
    _w = jnp.asarray

    def _L0_attn_setup():
        import jax, jax.numpy as jnp
        import numpy as np
        N_HEADS = 16
        ROPE_BASE = 10000.0

        def _rope(x):
            B, L, H, Dh = x.shape
            half = Dh // 2
            inv_freq = 1.0 / ROPE_BASE ** (jnp.arange(0, half, dtype=jnp.float32) / half)
            ang = jnp.arange(L, dtype=jnp.float32)[:, None] * inv_freq[None, :]
            cos = jnp.concatenate([jnp.cos(ang), jnp.cos(ang)], axis=-1).astype(x.dtype)
            sin = jnp.concatenate([jnp.sin(ang), jnp.sin(ang)], axis=-1).astype(x.dtype)
            cos = cos[None, :, None, :]
            sin = sin[None, :, None, :]
            x1, x2 = (x[..., :half], x[..., half:])
            rot = jnp.concatenate([-x2, x1], axis=-1)
            return x * cos + rot * sin
        key = jax.random.key(seed)
        k1, k2, k3 = jax.random.split(key, 3)
        B, L, D = (2, 512, 256)
        x = jax.random.normal(k1, (B, L, D), dtype=jnp.float32)
        w_qkv = jax.random.normal(k2, (3 * D, D), dtype=jnp.float32) * D ** (-0.5)
        w_out = jax.random.normal(k3, (D, D), dtype=jnp.float32) * D ** (-0.5)
        return {'x': x, 'w_qkv': w_qkv, 'w_out': w_out}
    _L0_attn_in = _L0_attn_setup()

    def _L0_ffn_setup():
        import jax, jax.numpy as jnp
        import numpy as np
        DIM = 256
        DEPTH = 2
        HEADS = 8
        DIM_HEAD = 64
        WINDOW = 128
        INNER = HEADS * DIM_HEAD
        HID = int(DIM * 4 * 2 / 3)
        B, N = (2, 2048)
        QK_SCALE = 8.0

        def shift_token(t):
            t1, t2 = jnp.split(t, 2, axis=-1)
            t2 = jnp.pad(t2, ((0, 0), (1, 0), (0, 0)))[:, :-1]
            return jnp.concatenate([t1, t2], axis=-1)

        def l2norm(t):
            return t / jnp.clip(jnp.linalg.norm(t, axis=-1, keepdims=True), 1e-12)

        def rotate_half(x):
            x1, x2 = jnp.split(x, 2, axis=-1)
            return jnp.concatenate([-x2, x1], axis=-1)

        def rotary_xpos(q, k):
            n = q.shape[-2]
            half_idx = jnp.arange(0, DIM_HEAD, 2, dtype=jnp.float32)
            inv_freq = 1.0 / 10000.0 ** (half_idx / DIM_HEAD)
            t = jnp.arange(n, dtype=jnp.float32)
            freqs = t[:, None] * inv_freq[None, :]
            freqs = jnp.concatenate([freqs, freqs], axis=-1)
            base = (half_idx + 0.4 * DIM_HEAD) / (1.4 * DIM_HEAD)
            power = (t - n // 2) / float(WINDOW // 2)
            scale = base[None, :] ** power[:, None]
            scale = jnp.concatenate([scale, scale], axis=-1)
            cos, sin = (jnp.cos(freqs), jnp.sin(freqs))
            q = q * cos * scale + rotate_half(q) * sin * scale
            k = k * cos / scale + rotate_half(k) * sin / scale
            return (q, k)

        def local_attention(q, k, v):
            b, h, n, d = q.shape
            w = n // WINDOW
            bq = q.reshape(b, h, w, WINDOW, d) * QK_SCALE
            bk = k.reshape(b, h, w, WINDOW, d)
            bv = v.reshape(b, h, w, WINDOW, d)

            def look_around(t):
                p = jnp.pad(t, ((0, 0), (0, 0), (1, 0), (0, 0), (0, 0)))
                return jnp.concatenate([p[:, :, :w], p[:, :, 1:]], axis=3)
            bk, bv = (look_around(bk), look_around(bv))
            bt = jnp.arange(n).reshape(w, WINDOW)
            btp = jnp.pad(bt, ((1, 0), (0, 0)), constant_values=-1)
            btk = jnp.concatenate([btp[:w], btp[1:]], axis=1)
            sim = jnp.einsum('bhwid,bhwjd->bhwij', bq, bk)
            i = bt[:, :, None]
            j = btk[:, None, :]
            mask = (i < j) | (i > j + WINDOW) | (j == -1)
            sim = jnp.where(mask, -jnp.finfo(sim.dtype).max, sim)
            attn = jax.nn.softmax(sim, axis=-1)
            out = jnp.einsum('bhwij,bhwjd->bhwid', attn, bv)
            return out.reshape(b, h, n, d)

        def _layer(x, wqkv, qs, ksc, wo, lg, lb, w1, b1, w2, b2):
            b, n, _ = x.shape
            h = shift_token(x)
            qkv = h @ wqkv
            q, k, v = jnp.split(qkv, 3, axis=-1)
            to_heads = lambda t: t.reshape(b, n, HEADS, DIM_HEAD).transpose(0, 2, 1, 3)
            q, k, v = (to_heads(q), to_heads(k), to_heads(v))
            q = l2norm(q) * qs
            k = l2norm(k) * ksc
            q, k = rotary_xpos(q, k)
            o = local_attention(q, k, v)
            o = o.transpose(0, 2, 1, 3).reshape(b, n, INNER)
            x = x + o @ wo
            h = shift_token(x)
            mu = h.mean(-1, keepdims=True)
            var = h.var(-1, keepdims=True)
            h = (h - mu) / jnp.sqrt(var + 1e-05) * lg + lb
            h = h @ w1 + b1
            a, g = jnp.split(h, 2, axis=-1)
            h = a * jax.nn.gelu(g, approximate=False)
            x = x + h @ w2 + b2
            return x
        key = jax.random.key(seed)
        ks = jax.random.split(key, 6)
        return {'x': jax.random.normal(ks[0], (B, N, DIM), jnp.float32), 'wqkv': jax.random.normal(ks[1], (DEPTH, DIM, 3 * INNER), jnp.float32) * 0.02, 'q_scale': jnp.ones((DEPTH, DIM_HEAD), jnp.float32), 'k_scale': jnp.ones((DEPTH, DIM_HEAD), jnp.float32), 'wo': jax.random.normal(ks[2], (DEPTH, INNER, DIM), jnp.float32) * 0.02, 'ln_g': jnp.ones((DEPTH, DIM), jnp.float32), 'ln_b': jnp.zeros((DEPTH, DIM), jnp.float32), 'w1': jax.random.normal(ks[3], (DEPTH, DIM, 2 * HID), jnp.float32) * 0.02, 'b1': jnp.zeros((DEPTH, 2 * HID), jnp.float32), 'w2': jax.random.normal(ks[4], (DEPTH, HID, DIM), jnp.float32) * 0.02, 'b2': jnp.zeros((DEPTH, DIM), jnp.float32)}
    _L0_ffn_in = _L0_ffn_setup()
    _d = {'L0_attn_x': _L0_attn_in['x'], 'L0_attn_w_qkv': _L0_attn_in['w_qkv'], 'L0_attn_w_out': _L0_attn_in['w_out'], 'L0_ffn_wqkv': _L0_ffn_in['wqkv'], 'L0_ffn_q_scale': _L0_ffn_in['q_scale'], 'L0_ffn_k_scale': _L0_ffn_in['k_scale'], 'L0_ffn_wo': _L0_ffn_in['wo'], 'L0_ffn_ln_g': _L0_ffn_in['ln_g'], 'L0_ffn_ln_b': _L0_ffn_in['ln_b'], 'L0_ffn_w1': _L0_ffn_in['w1'], 'L0_ffn_b1': _L0_ffn_in['b1'], 'L0_ffn_w2': _L0_ffn_in['w2'], 'L0_ffn_b2': _L0_ffn_in['b2']}
    _x0 = _d['L0_attn_x']
    _d['L0_attn_x'] = jax.random.normal(jax.random.fold_in(jax.random.key(seed), 1), (16, 512, 256), dtype=_x0.dtype)
    del _x0
    return _d

def reference(L0_attn_x, L0_attn_w_qkv, L0_attn_w_out, L0_ffn_wqkv, L0_ffn_q_scale, L0_ffn_k_scale, L0_ffn_wo, L0_ffn_ln_g, L0_ffn_ln_b, L0_ffn_w1, L0_ffn_b1, L0_ffn_w2, L0_ffn_b2):

    def _L0_attn_ref(x, w_qkv, w_out):
        import jax, jax.numpy as jnp
        import numpy as np
        N_HEADS = 16
        ROPE_BASE = 10000.0

        def _rope(x):
            B, L, H, Dh = x.shape
            half = Dh // 2
            inv_freq = 1.0 / ROPE_BASE ** (jnp.arange(0, half, dtype=jnp.float32) / half)
            ang = jnp.arange(L, dtype=jnp.float32)[:, None] * inv_freq[None, :]
            cos = jnp.concatenate([jnp.cos(ang), jnp.cos(ang)], axis=-1).astype(x.dtype)
            sin = jnp.concatenate([jnp.sin(ang), jnp.sin(ang)], axis=-1).astype(x.dtype)
            cos = cos[None, :, None, :]
            sin = sin[None, :, None, :]
            x1, x2 = (x[..., :half], x[..., half:])
            rot = jnp.concatenate([-x2, x1], axis=-1)
            return x * cos + rot * sin
        B, L, D = x.shape
        H = N_HEADS
        Dh = D // H
        qkv = jnp.einsum('bld,ed->ble', x, w_qkv)
        q, k, v = jnp.split(qkv, 3, axis=-1)
        q = q.reshape(B, L, H, Dh)
        k = k.reshape(B, L, H, Dh)
        v = v.reshape(B, L, H, Dh)
        q = _rope(q)
        k = _rope(k)
        scale = 1.0 / jnp.sqrt(jnp.asarray(Dh, dtype=x.dtype))
        scores = jnp.einsum('blhd,bmhd->bhlm', q, k) * scale
        attn = jax.nn.softmax(scores, axis=-1)
        out = jnp.einsum('bhlm,bmhd->blhd', attn, v).reshape(B, L, D)
        return jnp.einsum('bld,ed->ble', out, w_out)

    def _L0_ffn_ref(x, wqkv, q_scale, k_scale, wo, ln_g, ln_b, w1, b1, w2, b2):
        import jax, jax.numpy as jnp
        import numpy as np
        DIM = 256
        DEPTH = 2
        HEADS = 8
        DIM_HEAD = 64
        WINDOW = 128
        INNER = HEADS * DIM_HEAD
        HID = int(DIM * 4 * 2 / 3)
        B, N = (2, 2048)
        QK_SCALE = 8.0

        def shift_token(t):
            t1, t2 = jnp.split(t, 2, axis=-1)
            t2 = jnp.pad(t2, ((0, 0), (1, 0), (0, 0)))[:, :-1]
            return jnp.concatenate([t1, t2], axis=-1)

        def l2norm(t):
            return t / jnp.clip(jnp.linalg.norm(t, axis=-1, keepdims=True), 1e-12)

        def rotate_half(x):
            x1, x2 = jnp.split(x, 2, axis=-1)
            return jnp.concatenate([-x2, x1], axis=-1)

        def rotary_xpos(q, k):
            n = q.shape[-2]
            half_idx = jnp.arange(0, DIM_HEAD, 2, dtype=jnp.float32)
            inv_freq = 1.0 / 10000.0 ** (half_idx / DIM_HEAD)
            t = jnp.arange(n, dtype=jnp.float32)
            freqs = t[:, None] * inv_freq[None, :]
            freqs = jnp.concatenate([freqs, freqs], axis=-1)
            base = (half_idx + 0.4 * DIM_HEAD) / (1.4 * DIM_HEAD)
            power = (t - n // 2) / float(WINDOW // 2)
            scale = base[None, :] ** power[:, None]
            scale = jnp.concatenate([scale, scale], axis=-1)
            cos, sin = (jnp.cos(freqs), jnp.sin(freqs))
            q = q * cos * scale + rotate_half(q) * sin * scale
            k = k * cos / scale + rotate_half(k) * sin / scale
            return (q, k)

        def local_attention(q, k, v):
            b, h, n, d = q.shape
            w = n // WINDOW
            bq = q.reshape(b, h, w, WINDOW, d) * QK_SCALE
            bk = k.reshape(b, h, w, WINDOW, d)
            bv = v.reshape(b, h, w, WINDOW, d)

            def look_around(t):
                p = jnp.pad(t, ((0, 0), (0, 0), (1, 0), (0, 0), (0, 0)))
                return jnp.concatenate([p[:, :, :w], p[:, :, 1:]], axis=3)
            bk, bv = (look_around(bk), look_around(bv))
            bt = jnp.arange(n).reshape(w, WINDOW)
            btp = jnp.pad(bt, ((1, 0), (0, 0)), constant_values=-1)
            btk = jnp.concatenate([btp[:w], btp[1:]], axis=1)
            sim = jnp.einsum('bhwid,bhwjd->bhwij', bq, bk)
            i = bt[:, :, None]
            j = btk[:, None, :]
            mask = (i < j) | (i > j + WINDOW) | (j == -1)
            sim = jnp.where(mask, -jnp.finfo(sim.dtype).max, sim)
            attn = jax.nn.softmax(sim, axis=-1)
            out = jnp.einsum('bhwij,bhwjd->bhwid', attn, bv)
            return out.reshape(b, h, n, d)

        def _layer(x, wqkv, qs, ksc, wo, lg, lb, w1, b1, w2, b2):
            b, n, _ = x.shape
            h = shift_token(x)
            qkv = h @ wqkv
            q, k, v = jnp.split(qkv, 3, axis=-1)
            to_heads = lambda t: t.reshape(b, n, HEADS, DIM_HEAD).transpose(0, 2, 1, 3)
            q, k, v = (to_heads(q), to_heads(k), to_heads(v))
            q = l2norm(q) * qs
            k = l2norm(k) * ksc
            q, k = rotary_xpos(q, k)
            o = local_attention(q, k, v)
            o = o.transpose(0, 2, 1, 3).reshape(b, n, INNER)
            x = x + o @ wo
            h = shift_token(x)
            mu = h.mean(-1, keepdims=True)
            var = h.var(-1, keepdims=True)
            h = (h - mu) / jnp.sqrt(var + 1e-05) * lg + lb
            h = h @ w1 + b1
            a, g = jnp.split(h, 2, axis=-1)
            h = a * jax.nn.gelu(g, approximate=False)
            x = x + h @ w2 + b2
            return x
        for l in range(DEPTH):
            x = _layer(x, wqkv[l], q_scale[l], k_scale[l], wo[l], ln_g[l], ln_b[l], w1[l], b1[l], w2[l], b2[l])
        return x
    x = L0_attn_x
    xn = _layernorm(x, axis=-1)
    x = x + _L0_attn_ref(xn, L0_attn_w_qkv, L0_attn_w_out) + _L0_ffn_ref(xn, L0_ffn_wqkv, L0_ffn_q_scale, L0_ffn_k_scale, L0_ffn_wo, L0_ffn_ln_g, L0_ffn_ln_b, L0_ffn_w1, L0_ffn_b1, L0_ffn_w2, L0_ffn_b2)
    return x

_drawn_inputs = setup_inputs


def setup_inputs(seed=0):
    import zlib

    import numpy as np

    out = dict(_drawn_inputs(seed))
    spreads = {'L0_ffn_q_scale': (1.0, 0.6),
     'L0_ffn_k_scale': (1.0, 0.6),
     'L0_ffn_ln_g': (1.0, 0.6),
     'L0_ffn_ln_b': (0.0, 0.8),
     'L0_ffn_b1': (0.0, 0.8),
     'L0_ffn_b2': (0.0, 0.1)}
    factors = {'L0_ffn_wqkv': 3.031, 'L0_ffn_wo': 2.993}
    for name, (base, spread) in spreads.items():
        noise = np.random.default_rng([zlib.crc32(name.encode()), seed]).standard_normal(out[name].shape)
        drawn = base * np.exp(spread * noise) if base else spread * noise
        out[name] = jnp.asarray(drawn.astype(out[name].dtype))
    for name, factor in factors.items():
        out[name] = (out[name] * factor).astype(out[name].dtype)
    return out
```

```python
from contextlib import ExitStack

import numpy as np

import concourse.bass as bass
from concourse import mybir

ALU = mybir.AluOpType
ACT = mybir.ActivationFunctionType
AX = mybir.AxisListType
F32, F16, BF16, I32 = mybir.dt.float32, mybir.dt.float16, mybir.dt.bfloat16, mybir.dt.int32

P = 128
WSCALE = 1024.0
KBOOST = 32.0
EPS = 1e-5
NORM_MIN = 1e-12
MASKED = -1e30
MAGIC = float(0x5F3759DF)


class Signal:

    def __init__(self, sem, name, per):
        self.sem, self.name, self.per, self.seen = sem, name, per, {}

    def up(self, I, n=1):
        self.seen[I.id] = self.seen.get(I.id, 0) + n
        return self.sem, n

    def at(self, I, n):
        return self.sem, I.b * self.per + (n + 1)

    def now(self, I):
        return self.at(I, self.seen[I.id])

    def before(self, I, k):
        return self.sem, (I.b - (k - 1)) * self.per + 1


class Inst:

    def __init__(self, id, par, add, first=False):
        self.id, self.par, self.add, self.first, self.b = id, par, add, first, None


class Section:
    def __init__(self, name, steps, loop=None):
        self.name, self.steps, self.loop = name, steps, loop


class PsumPlan:

    def __init__(self, pools, sections, tiles_of, outer):
        slots = [s for p in pools.values() for s in p]
        self.tile, fills, frees = {}, dict.fromkeys(slots, 0), dict.fromkeys(slots, 0)
        self.per_loop = {}
        for sec in sections:
            queue = {p: list(s) for p, s in pools.items()}
            f0, e0 = dict(fills), dict(frees)
            for step in sec.steps:
                for key, pool, n_free in tiles_of(step):
                    if n_free is None:
                        s = self.tile[(sec.name, step[1].id) + key][0]
                    else:
                        s = queue[pool][0]
                    queue[pool].remove(s)
                    queue[pool].append(s)
                    if n_free is None:
                        continue
                    self.tile[(sec.name, step[1].id) + key] = (s, fills[s], frees[s], n_free)
                    fills[s] += 1
                    frees[s] += n_free
            rounds = sec.loop[1] - sec.loop[0] if sec.loop else 1
            self.per_loop[sec.name] = {s: (fills[s] - f0[s], frees[s] - e0[s]) for s in slots}
            for s in slots:
                fills[s] = f0[s] + rounds * (fills[s] - f0[s])
                frees[s] = e0[s] + rounds * (frees[s] - e0[s])
        self.per_outer = {s: (fills[s], frees[s]) for s in slots}


def merge(a, b):
    def timed(steps):
        total = float(sum(c for _, c in steps)) or 1.0
        t, out = 0.0, []
        for s, c in steps:
            out.append(((t + c / 2) / total, s))
            t += c
        return out
    both = [(t, 0, i, s) for i, (t, s) in enumerate(timed(a))] + [(t, 1, i, s) for i, (t, s) in enumerate(timed(b))]
    return [s for _, _, _, s in sorted(both, key=lambda x: x[:3])]


class Phase:

    def __init__(self, nc, ctx, name, counts, pools, sections, tiles_of, outer=1):
        self.nc, self.ctx, self.name, self.counts = nc, ctx, name, counts
        self.sections, self.outer = sections, outer
        self.plan = PsumPlan(pools, sections, tiles_of, outer)
        self.signals = {}
        slots = [s for p in pools.values() for s in p]
        self.full = {s: ctx.enter_context(nc.semaphore(f"{name}_full_{s}")) for s in slots}
        self.free = {s: ctx.enter_context(nc.semaphore(f"{name}_free_{s}")) for s in slots}

    def new_signal(self, name):
        s = Signal(self.ctx.enter_context(self.nc.semaphore(f"{self.name}_{name}")), name,
                   self.counts.get((self.name, name), 1))
        self.signals[name] = s
        return s

    def start_credits(self, eng):
        for s in list(self.signals.values()):
            eng.sem_inc(s.sem, 1)
        for s in list(self.full.values()) + list(self.free.values()):
            eng.sem_inc(s, 1)

    def measured(self):
        out = {}
        for n, s in self.signals.items():
            seen = set(s.seen.values())
            assert len(seen) == 1, (n, s.seen)
            out[(self.name, n)] = seen.pop()
        return out


class At(tuple):

    def __new__(cls, at, count):
        self = super().__new__(cls, at)
        self.count = count
        return self


class Walk:

    def __init__(self, phase, eng, batches_per_outer=0):
        self.ph, self.eng, self.bpo = phase, eng, batches_per_outer

    def run(self, steps, layer=None):
        for sec in self.ph.sections:
            if sec.loop:
                with self.eng.Fori(sec.loop[0], sec.loop[1]) as i:
                    self.body(sec, steps, i, layer)
            else:
                self.body(sec, steps, None, layer)

    def body(self, sec, steps, i, layer):
        self.sec, self.i, self.layer = sec, i, layer
        for step in sec.steps:
            kind, I, *args = step
            if kind not in steps:
                continue
            I.b = I.add(i)
            I.local = I.b
            if layer is not None:
                I.b = I.b + layer * self.bpo
            self.I = I
            steps[kind](I, *args)

    def _count(self, s, base, which):
        v = base
        if self.sec.loop:
            v = v + (self.i - self.sec.loop[0]) * self.ph.plan.per_loop[self.sec.name][s][which]
        if self.layer is not None:
            v = v + self.layer * self.ph.plan.per_outer[s][which]
        return v

    def is_full(self, *key):
        s, fills, _, _ = self.ph.plan.tile[(self.sec.name, self.I.id) + key]
        return At((self.ph.full[s], self._count(s, fills, 0) + 2), fills)

    def is_free(self, *key):
        s, _, frees, _ = self.ph.plan.tile[(self.sec.name, self.I.id) + key]
        return At((self.ph.free[s], self._count(s, frees, 1) + 1), frees)

    def is_drained(self, *key):
        s, _, frees, n_free = self.ph.plan.tile[(self.sec.name, self.I.id) + key]
        return At((self.ph.free[s], self._count(s, frees + n_free, 1) + 1), frees + n_free)

    def wait(self, a, b):
        if a[0] is b[0]:
            self.eng.wait_ge(*max(a, b, key=lambda at: at.count))
        else:
            self.eng.wait_ge(*a)
            self.eng.wait_ge(*b)

    def fills(self, *key):
        return self.ph.full[self.slot(*key)], 1

    def frees(self, *key):
        return self.ph.free[self.slot(*key)], 1

    def slot(self, *key):
        return self.ph.plan.tile[(self.sec.name, self.I.id) + key][0]


def rsqrt(dve, link, v, y, t):
    link(dve.tensor_scalar(t.bitcast(I32), v.bitcast(I32), 1, None, ALU.logical_shift_right))
    link(dve.tensor_scalar(y.bitcast(I32), t.bitcast(I32), -1.0, MAGIC, ALU.mult, ALU.add))
    for _ in range(3):
        link(dve.tensor_tensor(t, y, y, ALU.mult))
        link(dve.scalar_tensor_tensor(t, t, -0.5, v, ALU.mult, ALU.mult))
        link(dve.scalar_tensor_tensor(y, t, 1.5, y, ALU.add, ALU.mult))


def rope_tables(T, H):
    Dh = H
    half = Dh // 2
    inv = (np.float32(1.0) / np.float32(10000.0) ** (np.arange(half, dtype=np.float32) / np.float32(half))).astype(np.float32)
    ang = (np.arange(T, dtype=np.float32)[:, None] * inv[None, :]).astype(np.float64)
    c = np.concatenate([np.cos(ang)] * 2, -1)
    s = np.concatenate([-np.sin(ang), np.sin(ang)], -1)
    sc = np.array([Dh ** -0.5, 1.0])[None, :, None] / WSCALE
    return (c[:, None, :] * sc).astype(np.float32), (s[:, None, :] * sc).astype(np.float32)


def xpos_tables(T, Dh, window, q_scale):
    f32 = np.float32
    idx = np.arange(0, Dh, 2, dtype=f32)
    inv = (f32(1.0) / f32(10000.0) ** (idx / f32(Dh))).astype(f32)
    t = np.arange(T, dtype=f32)
    ang = (t[:, None] * inv[None, :]).astype(np.float64)
    base = ((idx + f32(0.4 * Dh)) / f32(1.4 * Dh)).astype(np.float64)
    power = ((t - T // 2) / f32(window // 2)).astype(np.float64)
    scale = base[None, :] ** power[:, None]
    scale = np.concatenate([scale, scale], -1)
    c = np.concatenate([np.cos(ang)] * 2, -1)
    s = np.concatenate([-np.sin(ang), np.sin(ang)], -1)
    m = np.stack([scale * q_scale, KBOOST / scale], 1)
    return (c[:, None, :] * m).astype(f32), (s[:, None, :] * m).astype(f32)


def stop(sp, at, held):
    sp.wait_ge(*at)
    sp.sem_inc(held, 1)


def identities(pool, done, mats):
    for m in mats:
        pool.memset(m[:], 0.0).then_inc(done, 1)
    pool.wait_ge(done, len(mats))
    for m in mats:
        pool.affine_select(out=m[:], in_=m[:], compare_op=ALU.not_equal, fill=1.0, base=0,
                           pattern=[[-1, P]], channel_multiplier=1).then_inc(done, 1)


def full_attention_phase(nc, counts, x, w_qkv, w_out, out, attn_res):
    B, T, D = x.shape
    NT, NC = T // P, D // P
    H = 16
    DH = D // H
    HG = 4
    NG = H // HG
    VW = P // HG
    SW = 4 * DH + 2
    cos, sin = rope_tables(T, DH)
    cos_d = nc.inline_tensor(cos, name="rope_cos").ap()
    sin_d = nc.inline_tensor(sin, name="rope_sin").ap()

    last = B - 1
    def stream_a(I):
        s = [(("LN", I), 1), (("XT", I), 2), (("MQ", I, 0), 3), (("MQ", I, 1), 3)]
        for t in range(2, NT):
            s += [(("MS", I, t - 2), 3), (("MQ", I, t), 3)]
        return s + [(("MS", I, NT - 2), 3), (("MS", I, NT - 1), 3)]

    def stream_b(I):
        s = []
        for h in range(HG):
            s.append((("M1", I, h), 2))
        for g in range(NG):
            s.append((("MM", I, g), 1))
            nxt = [(("M1", I, h), 2) for h in range((g + 1) * HG, min((g + 2) * HG, H))]
            if g > 0:
                s.append((("MO", I, g - 1), 1))
            for kt in range(NT):
                if kt < len(nxt):
                    s.append(nxt[kt])
                s.append((("M2", I, g, kt), 2))
                if kt > 0:
                    s.append((("MV", I, g, kt - 1), 2))
            s.append((("MV", I, g, NT - 1), 2))
        return s + [(("MO", I, NG - 1), 1), (("MT", I), 1), (("MP", I), 3)]

    a = lambda n, p, add, first=False: Inst(n, p, add, first)
    A0 = a("A0", 0, lambda i: 0, True)
    sections = [
        Section("start", [s for s, _ in stream_a(A0)]),
        Section("pairs", merge(stream_b(a("B_even", 0, lambda i: i * 2)), stream_a(a("A_odd", 1, lambda i: i * 2 + 1)))
                + merge(stream_b(a("B_odd", 1, lambda i: i * 2 + 1)), stream_a(a("A_even", 0, lambda i: i * 2 + 2))),
                loop=(0, B // 2 - 1)),
        Section("end", merge(stream_b(a("B_last_even", 0, lambda i: last - 1)), stream_a(a("A_last", 1, lambda i: last)))
                + [s for s, _ in stream_b(a("B_last", 1, lambda i: last))]),
    ]
    pools = {"pair": ["p0", "p1", "p2"], "acc": ["o0", "o1"]}

    def tiles_of(step):
        kind, I, *r = step
        return {
            "XT": lambda: [(("XT",), "pair", 1)],
            "MQ": lambda: [(("MQ", *r), "pair", 2)],
            "MS": lambda: [(("MSk", *r), "pair", 1), (("MSq", *r), "pair", 1)],
            "M1": lambda: [(("M1", *r, u), "pair", 1) for u in range(NT // 2)],
            "MM": lambda: [(("MM", *r), "pair", 1)],
            "M2": lambda: [(("M2", *r, u), "pair", 1) for u in range(HG // 2)],
            "MV": lambda: [(("MV", r[0]), "acc", 1)] if r[1] == 0 else [],
            "MO": lambda: [(("MO", *r), "pair", 1)],
            "MT": lambda: [(("MT",), "pair", 1)],
            "MP": lambda: [(("MP",), "pair", 1)],
        }.get(kind, lambda: [])()

    with ExitStack() as ctx:
        def sb(name, shape, dt):
            return ctx.enter_context(nc.sbuf_tensor("m_" + name, shape, dt))

        ph = Phase(nc, ctx, "m", counts, pools, sections, tiles_of)
        psum = {s: ctx.enter_context(nc.psum_tensor("m_" + s, [P, 1024], F32)) for s in pools["pair"]}
        psum |= {s: ctx.enter_context(nc.psum_tensor("m_" + s, [P, 512], F32)) for s in pools["acc"]}

        wq_h, wq_l = sb("wq_h", [P, NC, 3 * D], F16), sb("wq_l", [P, NC, 3 * D], F16)
        wo_h, wo_l = sb("wo_h", [P, NC, D], F16), sb("wo_l", [P, NC, D], F16)
        cos_t, sin_t = sb("cos", [P, NT, 2, DH], F32), sb("sin", [P, NT, 2, DH], F32)
        ident, identf = sb("ident", [P, P], F16), sb("identf", [P, P], F32)
        xin = [sb(f"xin{p}", [P, NT, D], F32) for p in range(2)]
        res, xn = sb("res", [P, NT, D], F32), sb("xn", [P, NT, D], F32)
        stats, mv = sb("stats", [P, NT, 6], F32), sb("mv", [P, NT, 2], F32)
        var, rstd, tmp = sb("var", [P, NT], F32), sb("rstd", [P, NT], F32), sb("tmp", [P, NT], F32)
        xT_h, xT_l = sb("xT_h", [P, NC, T], F16), sb("xT_l", [P, NC, T], F16)
        rc, rs = [[sb(f"{n}{r}", [P, 2 * D], F32) for r in range(2)] for n in ("rc", "rs")]
        qst, kst = [[sb(f"{n}{r}", [P, H, SW], F16) for r in range(2)] for n in ("qst", "kst")]
        QT, KT = [[sb(f"{n}{p}", [P, H, T], F16) for p in range(2)] for n in ("QT", "KT")]
        vm = [sb(f"vm{p}", [P, NT, H, VW], F32) for p in range(2)]
        negm, mT = sb("negm", [P, NT, H], F16), sb("mT", [HG, T], F16)
        Pr = [sb(f"Pr{r}", [P, HG, T], F32) for r in range(2)]
        OT = [sb(f"OT{r}", [P, T], F32) for r in range(2)]
        rden, on = sb("rden", [P, NT * HG], F32), sb("on", [P, NT, D], F32)
        oT_h, oT_l = sb("oT_h", [P, NC, T], F16), sb("oT_l", [P, NC, T], F16)
        mark_v, mark_a, mark_in = sb("mark_v", [1, 1], F32), sb("mark_a", [1, 1], F32), sb("mark_in", [1, 1], F32)
        stage_q = QT[1][:, :, :].rearrange("p h t -> p (h t)").bitcast(F32)[:, 0:NC * 3 * D].rearrange("p (c n) -> p c n", c=NC)
        stage_o = QT[1][:, :, :].rearrange("p h t -> p (h t)").bitcast(F32)[:, NC * 3 * D:NC * 4 * D].rearrange("p (c n) -> p c n", c=NC)

        x_loaded, xn_stored, res_stored = ph.new_signal("x_loaded"), ph.new_signal("xn_stored"), ph.new_signal("res_stored")
        ln_link, xn_ready = ph.new_signal("ln_link"), ph.new_signal("xn_ready")
        xT_h_ready, summed = ph.new_signal("xT_h_ready"), ph.new_signal("summed")
        split_link, stack_ready = ph.new_signal("split_link"), ph.new_signal("stack_ready")
        kv_ready, qT_ready = ph.new_signal("kv_ready"), ph.new_signal("qT_ready")
        mrow_done, pv_done = ph.new_signal("mrow_done"), ph.new_signal("pv_done")
        rden_ready, oT_h_ready = ph.new_signal("rden_ready"), ph.new_signal("oT_h_ready")
        w_loaded, zeroed = [ctx.enter_context(nc.semaphore("m_" + n)) for n in ("w_loaded", "zeroed")]
        w_hi, const_done = [ctx.enter_context(nc.semaphore("m_" + n)) for n in ("w_hi", "const_done")]
        sp_held = ctx.enter_context(nc.semaphore("m_sp_held"))
        w_lo, ident_done = [ctx.enter_context(nc.semaphore("m_" + n)) for n in ("w_lo", "ident_done")]

        x_v = x.rearrange("b (t p) d -> b p t d", p=P)
        out_v = out.rearrange("b (t p) d -> b p t d", p=P)
        res_v = attn_res.rearrange("b (t p) d -> b p t d", p=P)
        block = ctx.enter_context(nc.Block())

        @block.tensor
        def _(pe):
            w = Walk(ph, pe)
            pe.wait_ge(ident_done, 4)
            pe.wait_ge(const_done, 6)
            pe.wait_ge(w_lo, 2)

            def xt(I):
                pe.wait_ge(*xn_ready.at(I, NT))
                pe.wait_ge(*w.is_free("XT"))
                for c in range(NC):
                    for t in range(NT):
                        mm = pe.transpose(psum[w.slot("XT")][:, c * T + t * P:c * T + (t + 1) * P],
                                          xn[:, t, c * P:(c + 1) * P], identf[:])
                mm.then_inc(*w.fills("XT"))

            def mq(I, t):
                w.wait(w.is_drained("XT"), w.is_free("MQ", t))
                ps = psum[w.slot("MQ", t)]
                for n0, n1 in ((0, 2 * D), (2 * D, 3 * D)):
                    for c in range(NC):
                        for k, (a_, b_) in enumerate(((xT_h, wq_h), (xT_h, wq_l), (xT_l, wq_h))):
                            mm = pe.matmul(ps[:, n0:n1], a_[:, c, t * P:(t + 1) * P], b_[:, c, n0:n1],
                                           start=(c == 0 and k == 0), stop=(c == NC - 1 and k == 2))
                mm.then_inc(*w.fills("MQ", t))

            def ms(I, t):
                pe.wait_ge(*stack_ready.at(I, t + 1))
                for key, st in (("MSk", kst), ("MSq", qst)):
                    pe.wait_ge(*w.is_free(key, t))
                    ps = psum[w.slot(key, t)][:, :].bitcast(F16)
                    for h in range(H):
                        mm = pe.transpose(ps[0:4 * DH + 1, h * P:(h + 1) * P], st[t % 2][:, h, 0:4 * DH + 1], ident[:])
                    mm.then_inc(*w.fills(key, t))

            def m1(I, h):
                pe.wait_ge(*kv_ready.at(I, 1))
                pe.wait_ge(*qT_ready.at(I, 1))
                for u in range(NT // 2):
                    pe.wait_ge(*w.is_free("M1", h, u))
                    for v in range(2):
                        t = 2 * u + v
                        mm = pe.matmul(psum[w.slot("M1", h, u)][:, v * T:(v + 1) * T],
                                       QT[I.par][:, h, t * P:(t + 1) * P], KT[I.par][:, h, :], start=True, stop=True)
                    mm.then_inc(*w.fills("M1", h, u))

            def mmax(I, g):
                w.wait(w.is_drained("M1", (g + 1) * HG - 1, NT // 2 - 1), w.is_free("MM", g))
                ps = psum[w.slot("MM", g)][:, :].bitcast(F16)
                for t in range(NT):
                    mm = pe.transpose(ps[0:HG, t * P:(t + 1) * P], negm[:, t, g * HG:(g + 1) * HG], ident[:])
                mm.then_inc(*w.fills("MM", g))

            def m2(I, g, kt):
                pe.wait_ge(*mrow_done.at(I, 16 * (g + 1)))
                for u in range(HG // 2):
                    pe.wait_ge(*w.is_free("M2", g, kt, u))
                    for v in range(2):
                        h = g * HG + 2 * u + v
                        mm = pe.matmul(psum[w.slot("M2", g, kt, u)][:, v * T:(v + 1) * T],
                                       KT[I.par][:, h, kt * P:(kt + 1) * P], QT[I.par][:, h, :], start=True, stop=True)
                    mm.then_inc(*w.fills("M2", g, kt, u))

            def mv_(I, g, kt):
                if kt == 0:
                    pe.wait_ge(*w.is_free("MV", g))
                pe.wait_ge(*w.is_drained("M2", g, kt, HG // 2 - 1))
                for j in range(HG):
                    mm = pe.matmul(psum[w.slot("MV", g)][j * VW:(j + 1) * VW, :], vm[I.par][:, kt, g * HG + j, :],
                                   Pr[kt % 2][:, j, :], start=(kt == 0), stop=(kt == NT - 1))
                if kt == NT - 1:
                    mm.then_inc(*w.fills("MV", g))
                else:
                    mm.then_inc(*pv_done.up(I))

            def mo(I, g):
                w.wait(w.is_drained("MV", g), w.is_free("MO", g))
                for t in range(NT):
                    mm = pe.transpose(psum[w.slot("MO", g)][:, t * P:(t + 1) * P], OT[g % 2][:, t * P:(t + 1) * P], identf[:])
                mm.then_inc(*w.fills("MO", g))

            def mt(I):
                w.wait(w.is_drained("MO", NG - 1), w.is_free("MT"))
                for c in range(NC):
                    for t in range(NT):
                        mm = pe.transpose(psum[w.slot("MT")][:, c * T + t * P:c * T + (t + 1) * P],
                                          on[:, t, c * P:(c + 1) * P], identf[:])
                mm.then_inc(*w.fills("MT"))

            def mp(I):
                w.wait(w.is_drained("MT"), w.is_free("MP"))
                for t in range(NT):
                    for c in range(NC):
                        for k, (a_, b_) in enumerate(((oT_h, wo_h), (oT_h, wo_l), (oT_l, wo_h))):
                            mm = pe.matmul(psum[w.slot("MP")][:, t * D:(t + 1) * D], a_[:, c, t * P:(t + 1) * P],
                                           b_[:, c, :], start=(c == 0 and k == 0), stop=(c == NC - 1 and k == 2))
                mm.then_inc(*w.fills("MP"))

            w.run({"XT": xt, "MQ": mq, "MS": ms, "M1": m1, "MM": mmax, "M2": m2, "MV": mv_, "MO": mo, "MT": mt, "MP": mp})

        @block.scalar
        def _(act):
            w = Walk(ph, act)
            act.wait_ge(w_loaded, 16)
            act.activation(wq_h[:], stage_q, ACT.Copy, scale=WSCALE).then_inc(w_hi, 1)
            act.wait_ge(w_loaded, 32)
            act.activation(wo_h[:], stage_o, ACT.Copy, scale=WSCALE).then_inc(w_hi, 1)
            act.wait_ge(const_done, 6)
            act.wait_ge(zeroed, 5)

            def xt(I):
                act.wait_ge(*w.is_full("XT"))
                act.activation(xT_h[:].rearrange("p c t -> p (c t)"), psum[w.slot("XT")][:, :], ACT.Copy)\
                    .then_inc(*xT_h_ready.up(I))

            def mq(I, t):
                act.wait_ge(*w.is_full("MQ", t))
                act.activation(vm[I.par][:, t, :, 0:DH],
                               psum[w.slot("MQ", t)][:, 2 * D:3 * D].rearrange("p (h d) -> p h d", h=H),
                               ACT.Copy, scale=1 / WSCALE).then_inc(*w.frees("MQ", t))

            def ms(I, t):
                act.wait_ge(*w.is_full("MSk", t))
                act.activation(KT[I.par][0:4 * DH + 1, :, t * P:(t + 1) * P],
                               psum[w.slot("MSk", t)][:, :].bitcast(F16)[0:4 * DH + 1, :].rearrange("p (h t) -> p h t", h=H),
                               ACT.Copy).then_inc(*w.frees("MSk", t))
                if t == NT - 1:
                    act.activation(mark_a[:], mark_in[:], ACT.Copy).then_inc(*kv_ready.up(I))

            def mmax(I, g):
                act.wait_ge(*w.is_full("MM", g))
                act.wait_ge(*mrow_done.at(I, 16 * g))
                act.activation(mT[:], psum[w.slot("MM", g)][:, :].bitcast(F16)[0:HG, 0:T], ACT.Copy)\
                    .then_inc(*w.frees("MM", g))

            def m2(I, g, kt):
                n = g * NT + kt
                if n >= 2 and (n - 2) % NT < NT - 1:
                    g2, kt2 = divmod(n - 2, NT)
                    act.wait_ge(*pv_done.at(I, g2 * (NT - 1) + kt2 + 1))
                for u in range(HG // 2):
                    act.wait_ge(*w.is_full("M2", g, kt, u))
                    act.activation(Pr[kt % 2][:, 2 * u:2 * u + 2, :].rearrange("p h t -> p (h t)"),
                                   psum[w.slot("M2", g, kt, u)][:, :], ACT.Exp)\
                        .then_inc(*w.frees("M2", g, kt, u))

            def mv_(I, g, kt):
                if kt < NT - 1:
                    return
                act.wait_ge(*w.is_full("MV", g))
                act.activation(OT[g % 2][:], psum[w.slot("MV", g)][:, :], ACT.Copy)\
                    .then_inc(*w.frees("MV", g))

            def mt(I):
                act.wait_ge(*w.is_full("MT"))
                act.activation(oT_h[:].rearrange("p c t -> p (c t)"), psum[w.slot("MT")][:, :], ACT.Copy)\
                    .then_inc(*oT_h_ready.up(I))

            w.run({"XT": xt, "MQ": mq, "MS": ms, "MM": mmax, "M2": m2, "MV": mv_, "MT": mt})

        @block.vector
        def _(dve):
            w = Walk(ph, dve)
            dve.wait_ge(w_hi, 1)
            dve.scalar_tensor_tensor(wq_l[:], stage_q, WSCALE, wq_h[:], ALU.mult, ALU.subtract).then_inc(w_lo, 1)
            dve.wait_ge(w_hi, 2)
            dve.scalar_tensor_tensor(wo_l[:], stage_o, WSCALE, wo_h[:], ALU.mult, ALU.subtract).then_inc(w_lo, 1)
            dve.wait_ge(w_lo, 2)
            for i, m in enumerate((QT[0], QT[1], KT[0], KT[1])):
                dve.memset(m[64:P, :, :].rearrange("p h t -> p (h t)").bitcast(F32), 0.0).then_inc(const_done, 1)
            for m in vm:
                dve.memset(m[:], 1.0).then_inc(const_done, 1)
            dve.memset(mark_in[:], 0.0).then_inc(zeroed, 1)
            for r in range(2):
                dve.memset(qst[r][:, :, 4 * DH:SW], 0.0).then_inc(zeroed, 1)
                dve.memset(kst[r][:, :, 4 * DH:SW], 1.0).then_inc(zeroed, 1)
            dve.wait_ge(zeroed, 5)
            dve.wait_ge(w_loaded, 64)
            dve.wait_ge(const_done, 6)

            def ln(I):
                def link(ins):
                    ins.then_inc(*ln_link.up(I))
                    dve.wait_ge(*ln_link.now(I))
                dve.wait_ge(*x_loaded.at(I, 16))
                for t in range(NT):
                    ins = dve.bn_stats(stats[:, t, :], xin[I.par][:, t, :])
                link(ins)
                dve.memset(mark_v[:], 0.0)
                for t in range(NT):
                    ins = dve.bn_aggr(mv[:, t, :], stats[:, t, :])
                link(ins)
                link(dve.tensor_scalar(var[:], mv[:, :, 1], EPS, None, ALU.add))
                rsqrt(dve, link, var[:], rstd[:], tmp[:])
                if not I.first:
                    dve.wait_ge(*xn_stored.before(I, 1))
                for t in range(NT):
                    dve.tensor_scalar(xn[:, t, :], xin[I.par][:, t, :], mv[:, t, 0:1], rstd[:, t:t + 1],
                                      ALU.subtract, ALU.mult).then_inc(*xn_ready.up(I))

            def xt(I):
                dve.wait_ge(*xT_h_ready.at(I, 1))
                dve.tensor_tensor(xT_l[:].rearrange("p c t -> p (c t)"), psum[w.slot("XT")][:, :],
                                  xT_h[:].rearrange("p c t -> p (c t)"), ALU.subtract)\
                    .then_inc(*w.frees("XT"))

            def mq(I, t):
                dve.wait_ge(*w.is_full("MQ", t))
                ps = psum[w.slot("MQ", t)]
                for i in range(2):
                    dve.tensor_tensor(rc[t % 2][:, i * D:(i + 1) * D].rearrange("p (h d) -> p h d", h=H),
                                      ps[:, i * D:(i + 1) * D].rearrange("p (h d) -> p h d", h=H),
                                      cos_t[:, t, i:i + 1, :].to_broadcast([P, H, DH]), ALU.mult)
                    ins = dve.tensor_tensor(
                        rs[t % 2][:, i * D:(i + 1) * D].rearrange("p (h s d) -> p h s d", h=H, s=2),
                        ps[:, i * D:(i + 1) * D].rearrange("p (h s d) -> p h s d", h=H, s=2)[:, :, ::-1, :],
                        sin_t[:, t, i, :].rearrange("p (s d) -> p s d", s=2).unsqueeze(1).to_broadcast([P, H, 2, DH // 2]),
                        ALU.mult)
                ins.then_inc(*w.frees("MQ", t))

            def ms(I, t):
                r = t % 2
                dve.wait_ge(*summed.at(I, t + 1))
                def part(st, i):
                    return st[r][:, :, i * DH:(i + 1) * DH]
                src = rc[r][:].rearrange("p (i h d) -> p i h d", i=2, h=H)
                def two(st, i, step):
                    return st[r][:, :, 0:4 * DH].rearrange("p h (s d) -> p h s d", s=4)[:, :, i:i + step + 1:step, :]
                dve.tensor_copy(two(qst, 0, 1), src[:, 0].unsqueeze(2).to_broadcast([P, H, 2, DH])).then_inc(*split_link.up(I))
                dve.tensor_copy(two(kst, 0, 2), src[:, 1].unsqueeze(2).to_broadcast([P, H, 2, DH])).then_inc(*split_link.up(I))
                dve.wait_ge(*split_link.now(I))
                dve.tensor_tensor(part(qst, 2), src[:, 0], part(qst, 0), ALU.subtract).then_inc(*split_link.up(I))
                dve.tensor_tensor(part(kst, 1), src[:, 1], part(kst, 0), ALU.subtract).then_inc(*split_link.up(I))
                dve.wait_ge(*split_link.now(I))
                dve.tensor_copy(part(qst, 3), part(qst, 2))
                dve.tensor_copy(part(kst, 3), part(kst, 1)).then_inc(*stack_ready.up(I))
                dve.wait_ge(*w.is_full("MSq", t))
                dve.tensor_copy(QT[I.par][0:4 * DH + 1, :, t * P:(t + 1) * P],
                                psum[w.slot("MSq", t)][:, :].bitcast(F16)[0:4 * DH + 1, :].rearrange("p (h t) -> p h t", h=H))\
                    .then_inc(*w.frees("MSq", t))
                if t == NT - 1:
                    dve.memset(mark_v[:], 0.0).then_inc(*qT_ready.up(I))

            def m1(I, h):
                for u in range(NT // 2):
                    dve.wait_ge(*w.is_full("M1", h, u))
                    dve.tensor_reduce(negm[:, 2 * u:2 * u + 2, h], psum[w.slot("M1", h, u)][:, :].rearrange("p (a k) -> p a k", a=2),
                                      AX.X, ALU.max, negate=True).then_inc(*w.frees("M1", h, u))

            def mo(I, g):
                dve.wait_ge(*w.is_full("MO", g))
                ps = psum[w.slot("MO", g)][:, 0:T].rearrange("p (a v) -> p a v", v=VW)
                dve.reciprocal(rden[:], ps[:, :, DH]).then_inc(*rden_ready.up(I))
                dve.wait_ge(*rden_ready.now(I))
                dve.tensor_tensor(on[:, :, g * HG * DH:(g + 1) * HG * DH].rearrange("p t (j d) -> p t j d", j=HG),
                                  ps[:, :, 0:DH].rearrange("p (t j) d -> p t j d", j=HG),
                                  rden[:].rearrange("p (t j) -> p t j", j=HG).unsqueeze(3).to_broadcast([P, NT, HG, DH]),
                                  ALU.mult).then_inc(*w.frees("MO", g))

            def mt(I):
                dve.wait_ge(*oT_h_ready.at(I, 1))
                dve.tensor_tensor(oT_l[:].rearrange("p c t -> p (c t)"), psum[w.slot("MT")][:, :],
                                  oT_h[:].rearrange("p c t -> p (c t)"), ALU.subtract)\
                    .then_inc(*w.frees("MT"))

            def mp(I):
                dve.wait_ge(*w.is_full("MP"))
                dve.wait_ge(*res_stored.at(I, 0))
                dve.scalar_tensor_tensor(res[:].rearrange("p t d -> p (t d)"), psum[w.slot("MP")][:, :], 1 / WSCALE,
                                         xin[I.par][:].rearrange("p t d -> p (t d)"), ALU.mult, ALU.add)\
                    .then_inc(*w.frees("MP"))

            w.run({"LN": ln, "XT": xt, "MQ": mq, "MS": ms, "M1": m1, "MO": mo, "MT": mt, "MP": mp})

        @block.gpsimd
        def _(pool):
            w = Walk(ph, pool)
            identities(pool, ident_done, (ident, identf))

            def mq(I, t):
                pool.wait_ge(*w.is_drained("MQ", t))
                pool.tensor_tensor(rc[t % 2][:], rc[t % 2][:], rs[t % 2][:], ALU.add).then_inc(*summed.up(I))

            w.run({"MQ": mq})

        @block.sync
        def _(sp):
            hold = lambda at: stop(sp, at, sp_held)
            w = Walk(ph, sp)
            ph.start_credits(sp)
            sp.dma_start(stage_q, w_qkv.rearrange("(c p) n -> p c n", p=P)).then_inc(w_loaded, 16)
            sp.wait_ge(w_loaded, 16)
            sp.dma_start(stage_o, w_out.rearrange("(c p) n -> p c n", p=P)).then_inc(w_loaded, 16)
            sp.wait_ge(w_loaded, 32)
            sp.dma_start(cos_t[:], cos_d.rearrange("(t p) i d -> p t i d", p=P)).then_inc(w_loaded, 16)
            sp.dma_start(sin_t[:], sin_d.rearrange("(t p) i d -> p t i d", p=P)).then_inc(w_loaded, 16)

            def ln(I):
                if not I.first:
                    hold(res_stored.before(I, 2))
                sp.dma_start(xin[I.par][:], x_v[I.b]).then_inc(*x_loaded.up(I, 16))
                hold(xn_ready.at(I, NT))
                sp.dma_start(out_v[I.b], xn[:]).then_inc(*xn_stored.up(I, 16))

            def mmax(I, g):
                hold(w.is_drained("MM", g))
                sp.dma_start(QT[I.par][4 * DH:4 * DH + 1, g * HG:(g + 1) * HG, :], mT[:]).then_inc(*mrow_done.up(I, 16))

            def mp(I):
                hold(w.is_drained("MP"))
                sp.dma_start(res_v[I.b], res[:]).then_inc(*res_stored.up(I, 16))

            w.run({"LN": ln, "MM": mmax, "MP": mp})
            end = Inst("after", 0, None)
            end.b = B
            hold(xn_stored.at(end, 0))
            hold(res_stored.at(end, 0))

    return ph.measured()


def layers_phase(nc, counts, wqkv, q_scale, k_scale, wo, ln_g, ln_b, w1, b1, w2, b2, out, attn_res):
    B, T, D = out.shape
    L = wqkv.shape[0]
    NT, NC = T // P, D // P
    W = P
    INNER = wo.shape[1]
    H = 8
    DH = INNER // H
    NP_ = H // 2
    HID = w2.shape[1]
    NF = -(-HID // P)
    TAIL = HID - (NF - 1) * P
    NK = 2 * (NT - 1) * W + W
    base_cos, base_sin = xpos_tables(T, DH, W, 8.0)
    cos_d = nc.inline_tensor(base_cos, name="xpos_cos").ap()
    sin_d = nc.inline_tensor(base_sin, name="xpos_sin").ap()
    last_only = np.zeros((L, 1), np.float32)
    last_only[L - 1] = 1.0
    last_only_d = nc.inline_tensor(last_only, name="last_only").ap()
    RS = 13

    order = """A.XT F.W1,0 F.W1,1 A.QK,0 F.H1,0 F.W1,2 A.XR A.QK,1 F.H1,1 F.W1,3 A.SH,0 A.QK,2 F.H1,2 A.ST,0 F.W1,4 A.SH,1
               A.QK,3 F.H1,3 A.ST,1 F.W1,5 A.SH,2 F.H1,4 F.H1,5 A.ST,2 F.W2,0 A.SH,3 F.W2,1 A.ST,3 F.W2,2
               A.L1,0 A.L1,1 A.L1,2 A.L1,3 A.L1,4 A.L1,5 A.L1,6 A.L1,7 A.LM N.LS A.L2,0 A.L2,1
               A.L2,2 A.PV,0 A.L2,3 A.RD,0 A.L2,4 A.PV,1 A.RX,0 A.L2,5 A.RD,1 A.OL,0 N.LN A.L2,6 A.PV,2 A.RX,1 A.L2,7
               A.RD,2 A.OL,1 A.PV,3 A.RX,2 A.WO,0 A.RD,3 A.OL,2 N.XH A.WO,1 A.RX,3 A.WO,2 A.OL,3 A.WO,3""".split()

    def steps_of(**streams):
        found = []
        for word in order:
            stream, step = word.split(".")
            kind, *r = step.split(",")
            if stream in streams:
                found.append((kind, streams[stream], *[int(v) for v in r]))
        return found

    a = lambda n, add: Inst(n, 0, add)
    prep = a("prep", lambda i: 0)
    sections = [
        Section("weights", [("WB", prep)]),
        Section("first", steps_of(A=a("A_first", lambda i: 0))),
        Section("second", steps_of(A=a("A_second", lambda i: 1), N=a("N_second", lambda i: 0))),
        Section("rounds", steps_of(A=a("A", lambda i: i), N=a("N", lambda i: i - 1), F=a("F", lambda i: i - 2)), loop=(2, B)),
        Section("last", steps_of(N=a("N_last", lambda i: B - 1), F=a("F_late", lambda i: B - 2))
                + steps_of(F=a("F_last", lambda i: B - 1))),
    ]
    pools = {"pair": ["p0", "p1", "p2", "p3"]}

    def tiles_of(step):
        kind, I, *r = step
        return {
            "WB": lambda: [(("WB",), "pair", 1)],
            "XT": lambda: [(("XT",), "pair", 1)],
            "QK": lambda: [(("QK", *r), "pair", 1), (("V", *r), "pair", 1)],
            "ST": lambda: [(("STa", *r), "pair", 2), (("STb", *r), "pair", 1)],
            "L1": lambda: [(("L1", *r), "pair", 1)],
            "LM": lambda: [(("LM",), "pair", 1)],
            "L2": lambda: [(("L2", *r), "pair", 1)],
            "PV": lambda: [(("PV", *r), "pair", 1)],
            "RD": lambda: [(("RD", *r), "pair", 1)],
            "RX": lambda: [(("RX", *r), "pair", 1)],
            "WO": lambda: [(("WO",), "pair", 1 if r[0] == 0 else None)],
            "XH": lambda: [(("XH",), "pair", 1)],
            "W1": lambda: [(("W1", *r), "pair", 1)],
            "W2": lambda: [(("W2",), "pair", 1 if r[0] == 0 else None)],
        }.get(kind, lambda: [])()

    with ExitStack() as ctx:
        def sb(name, shape, dt):
            return ctx.enter_context(nc.sbuf_tensor("f_" + name, shape, dt))

        ph = Phase(nc, ctx, "f", counts, pools, sections, tiles_of, outer=L)
        psum = {s: ctx.enter_context(nc.psum_tensor("f_" + s, [P, 1024], F32)) for s in pools["pair"]}

        wq_h, wq_l = sb("wq_h", [P, NC, 3 * INNER], F16), sb("wq_l", [P, NC, 3 * INNER], F16)
        wo_h, wo_l = sb("wo_h", [P, NP_, D], F16), sb("wo_l", [P, NP_, D], F16)
        w1_h, w1_l = sb("w1_h", [P, NC, 2 * HID], F16), sb("w1_l", [P, NC, 2 * HID], F16)
        w2_h, w2_l = sb("w2_h", [P, NF, D], F16), sb("w2_l", [P, NF, D], F16)
        cos_t, sin_t = sb("cos", [P, NT, 2, DH], F32), sb("sin", [P, NT, 2, DH], F32)
        qk_scale, lng, lnb = sb("qk_scale", [P, 2, DH], F32), sb("lng", [P, NC], F32), sb("lnb", [P, NC], F32)
        b1_t, bias, b2_t = sb("b1", [P, 2, NF], F32), sb("bias", [P, 2, NF], F32), sb("b2", [P, D], F32)
        is_last = sb("is_last", [P, 1], F32)
        ident, identb, identf = sb("ident", [P, P], F16), sb("identb", [P, P], BF16), sb("identf", [P, P], F32)
        masks, mask0, sel = sb("masks", [P, 2, P], BF16), sb("mask0", [P, 2, P], BF16), sb("sel", [P, H, P], BF16)
        ones = sb("ones", [P, 32], F32)
        zeros = sb("zeros", [P, P], BF16)
        xs = sb("xs", [P, NT, D], F32)
        xT_h, xT_l = sb("xT_h", [P, NC, T + 2], F16), sb("xT_l", [P, NC, T + 2], F16)
        u = [sb(f"u{r}", [P, 2 * INNER], F32) for r in range(2)]
        bt, sq = sb("bt", [P, 2 * INNER], F32), sb("sq", [P, 2 * INNER], F32)
        ss, rn, rt = sb("ss", [P, 2 * H], F32), sb("rn", [P, 2 * H], F32), sb("rt", [P, 2 * H], F32)
        qst, khh, kll = [[sb(f"{n}{r}", [P, H, 2 * DH], F16) for r in range(2)] for n in ("qst", "khh", "kll")]
        qkt = sb("qkt", [P, 3, H, T], F16)
        QT, KH, KL = qkt[:, 0], qkt[:, 1], qkt[:, 2]
        vl = sb("vl", [P, NT, INNER], F32)
        negm, mT = sb("negm", [P, NT, H], BF16), sb("mT", [P, T], BF16)
        Pl = [sb(f"Pl{r}", [P, NK], F32) for r in range(4)]
        od = [sb(f"od{r}", [P, 2, T], F32) for r in range(2)]
        den, rden = sb("den", [P, NT, 2], F32), sb("rden", [P, NT, 2], F32)
        X = [sb(f"X{r}", [P, NT, 2, DH], F32) for r in range(2)]
        o = [sb(f"o{r}", [P, T], F32) for r in range(2)]
        oT_h, oT_l = sb("oT_h", [P, NP_, T], F16), sb("oT_l", [P, NP_, T], F16)
        x1, x1s, xb = sb("x1", [P, NT, D], F32), sb("x1s", [P, NT, D // 2], F32), sb("xb", [P, NT, D], F32)
        stats, mv = sb("stats", [P, NT, 2, 6], F32), sb("mv", [P, NT, 2], F32)
        var, rstd, tmp = sb("var", [P, NT], F32), sb("rstd", [P, NT], F32), sb("tmp", [P, NT], F32)
        xh = sb("xh", [P, NT, D], F32)
        xhT_h, xhT_l = sb("xhT_h", [P, NC, T], F16), sb("xhT_l", [P, NC, T], F16)
        G, hp_ = [[sb(f"{n}{r}", [P, T], F32) for r in range(2)] for n in ("G", "hp")]
        hT_h, hT_l = sb("hT_h", [P, NF, T], F16), sb("hT_l", [P, NF, T], F16)
        ar, xr = sb("ar", [P, NT, D], F32), sb("xr", [P, NT, D], F32)
        mark_v, mark_p = sb("mark_v", [1, 1], F32), sb("mark_p", [1, 1], F32)
        mark_x, mark_h = sb("mark_x", [1, 1], F32), sb("mark_h", [1, 1], F32)

        flat = qkt[:].rearrange("p a h t -> p (a h t)").bitcast(F32)
        n_q = NC * 3 * INNER
        st_q = flat[:, 0:n_q].rearrange("p (c n) -> p c n", c=NC)
        st_1 = flat[:, n_q:n_q + NC * 2 * HID].rearrange("p (c n) -> p c n", c=NC)
        st_2 = hT_h[:].rearrange("p f t -> p (f t)").bitcast(F32).rearrange("p (f n) -> p f n", f=NF)
        st_o = u[0][:].rearrange("p (f n) -> p f n", f=NP_)

        S = ph.new_signal
        w_loaded, w_hi, w_lo, w1_scaled, tables_done = S("w_loaded"), S("w_hi"), S("w_lo"), S("w1_scaled"), S("tables_done")
        x_loaded, xT_h_ready, sq_ready, q_link = S("x_loaded"), S("xT_h_ready"), S("sq_ready"), S("q_link")
        bt_used, u_ready, hi_ready, lo_link, stack_ready = S("bt_used"), S("u_ready"), S("hi_ready"), S("lo_link"), S("stack_ready")
        den_link, x_ready, oT_h_ready, oT_l_ready = S("den_link"), S("x_ready"), S("oT_h_ready"), S("oT_l_ready")
        x1_ready, shifted, ar_loaded, xb_ready, z_ready = S("x1_ready"), S("shifted"), S("ar_loaded"), S("xb_ready"), S("z_ready")
        ln_link, xh_ready, xhT_h_ready = S("ln_link"), S("xh_ready"), S("xhT_h_ready")
        g_ready, hh_ready, hl_ready, y_stored = S("g_ready"), S("hh_ready"), S("hl_ready"), S("y_stored")
        xT_ready, xhT_ready, xr_loaded = S("xT_ready"), S("xhT_ready"), S("xr_loaded")
        sp_held = ctx.enter_context(nc.semaphore("f_sp_held"))
        const_done, mask_zero, mask_done = [ctx.enter_context(nc.semaphore("f_" + n)) for n in ("const_done", "mask_zero", "mask_done")]
        N_CONST, N_MASK = 7, 9

        out_v = out.rearrange("b (t p) d -> b p t d", p=P)
        res_v = attn_res.rearrange("b (t p) d -> b p t d", p=P)
        block = ctx.enter_context(nc.Block())

        def layer_inst(layer):
            I = Inst("layer", 0, None)
            I.b = layer
            return I

        def rows(f):
            return P if f < NF - 1 else TAIL

        def hidden(g, f):
            return slice(g * HID + f * P, g * HID + f * P + rows(f))

        @block.tensor
        def _(pe):
            w = Walk(ph, pe, B)
            pe.wait_ge(const_done, N_CONST)
            pe.wait_ge(mask_done, N_MASK)

            def weight_bias(I):
                K = layer_inst(w.layer)
                pe.wait_ge(*w_loaded.at(K, w_loaded.per))
                pe.wait_ge(*w.is_free("WB"))
                for g in range(2):
                    for f in range(NF):
                        for c in range(NC):
                            mm = pe.matmul(psum[w.slot("WB")][0:rows(f), g * NF + f:g * NF + f + 1],
                                           st_1[:, c, hidden(g, f)], lnb[:, c:c + 1], start=(c == 0), stop=(c == NC - 1))
                mm.then_inc(*w.fills("WB"))
                pe.wait_ge(*w_lo.at(K, 4))
                pe.wait_ge(*tables_done.at(K, 4))

            def to_columns(key, src, ready):
                pe.wait_ge(*ready)
                pe.wait_ge(*w.is_free(key))
                for c in range(NC):
                    for t in range(NT):
                        mm = pe.transpose(psum[w.slot(key)][:, c * T + t * P:c * T + (t + 1) * P],
                                          src[:, t, c * P:(c + 1) * P], identf[:])
                mm.then_inc(*w.fills(key))

            def xt(I):
                to_columns("XT", xs, x_loaded.at(I, 16))

            def qk(I, t):
                pe.wait_ge(*xT_ready.at(I, 1))
                for key, cols in (("QK", (0, INNER)), ("V", (2 * INNER,))):
                    pe.wait_ge(*w.is_free(key, t))
                    for i, n0 in enumerate(cols):
                        for c in range(NC):
                            at = slice(t * P + 1 - c, (t + 1) * P + 1 - c)
                            for k, (a_, b_) in enumerate(((xT_h, wq_h), (xT_h, wq_l), (xT_l, wq_h))):
                                mm = pe.matmul(psum[w.slot(key, t)][:, i * INNER:(i + 1) * INNER], a_[:, c, at],
                                               b_[:, c, n0:n0 + INNER], start=(c == 0 and k == 0), stop=(c == NC - 1 and k == 2))
                    mm.then_inc(*w.fills(key, t))

            def st(I, t):
                r = t % 2
                pe.wait_ge(*stack_ready.at(I, t + 1))
                for key, parts in (("STa", (qst, khh)), ("STb", (kll,))):
                    pe.wait_ge(*w.is_free(key, t))
                    ps = psum[w.slot(key, t)][:, :].bitcast(F16)
                    for i, m in enumerate(parts):
                        for h in range(H):
                            mm = pe.transpose(ps[:, (i * H + h) * P:(i * H + h + 1) * P], m[r][:, h, :], ident[:])
                    mm.then_inc(*w.fills(key, t))

            def l1(I, h):
                w.wait(w.is_drained("STa", NT - 1), w.is_free("L1", h))
                ps = psum[w.slot("L1", h)]
                for n in range(NT):
                    lo = 1 if n == 0 else 0
                    pe.matmul(ps[:, 2 * n * W:2 * (n + 1) * W], identb[:], (mask0 if n == 0 else masks)[:].rearrange("p a k -> p (a k)"),
                              start=True, stop=False, skip_group_check=True)
                    mm = pe.matmul(ps[:, (2 * n + lo) * W:2 * (n + 1) * W], QT[:, h, n * W:(n + 1) * W],
                                   KH[:, h, (n - 1 + lo) * W:(n + 1) * W], start=False, stop=True, skip_group_check=True)
                mm.then_inc(*w.fills("L1", h))

            def lm(I):
                w.wait(w.is_drained("L1", H - 1), w.is_free("LM"))
                ps = psum[w.slot("LM")][:, :].bitcast(BF16)
                for t in range(NT):
                    mm = pe.transpose(ps[0:H, t * P:(t + 1) * P], negm[:, t, :], identb[:])
                mm.then_inc(*w.fills("LM"))

            def l2(I, h):
                w.wait(w.is_drained("LM"), w.is_free("L2", h))
                ps = psum[w.slot("L2", h)]
                mk = masks[:].rearrange("p a k -> p (a k)")
                for j in range(NT):
                    n = min(2 * W, T - j * W)
                    dst = ps[:, 2 * j * W:2 * j * W + n]
                    q = slice(j * W, j * W + n)
                    pe.matmul(dst, identb[:], mk[:, 0:n], start=True, stop=False, skip_group_check=True)
                    pe.matmul(dst, sel[:, h, :], mT[:, q], start=False, stop=False, skip_group_check=True)
                    pe.matmul(dst, KH[:, h, j * W:(j + 1) * W], QT[:, h, q], start=False, stop=False, skip_group_check=True)
                    mm = pe.matmul(dst, KL[:, h, j * W:(j + 1) * W], QT[:, h, q], start=False, stop=True, skip_group_check=True)
                mm.then_inc(*w.fills("L2", h))

            def pv(I, hp):
                w.wait(w.is_drained("L2", 2 * hp + 1), w.is_free("PV", hp))
                ps = psum[w.slot("PV", hp)]
                for j in range(NT):
                    n = min(2 * W, T - j * W)
                    for i in range(2):
                        h = 2 * hp + i
                        pe.matmul(ps[i * DH:(i + 1) * DH, j * W:j * W + n], vl[:, j, h * DH:(h + 1) * DH],
                                  Pl[h % 4][:, 2 * j * W:2 * j * W + n], start=(j == 0), stop=(j == NT - 1), skip_group_check=True)
                for i in range(2):
                    pe.matmul(ps[i * DH + 32:i * DH + 64, T:T + W], zeros[:, 0:32], zeros[:, :], start=True, stop=False,
                              skip_group_check=True)
                for j0 in range(0, NT, 2):
                    for i in range(2):
                        for j in (j0, j0 + 1):
                            n = min(2 * W, T - j * W)
                            r0 = i * DH + 32 * (j % 2)
                            mm = pe.matmul(ps[r0:r0 + 32, T + j * W:T + j * W + n], ones[:],
                                           Pl[(2 * hp + i) % 4][:, 2 * j * W:2 * j * W + n], start=(j == 0), stop=(j >= NT - 2),
                                           skip_group_check=True)
                mm.then_inc(*w.fills("PV", hp))

            def rd(I, hp):
                w.wait(w.is_drained("PV", hp), w.is_free("RD", hp))
                for t in range(NT):
                    mm = pe.transpose(psum[w.slot("RD", hp)][:, t * P:(t + 1) * P], od[hp % 2][:, 1, t * P:(t + 1) * P], identf[:])
                mm.then_inc(*w.fills("RD", hp))

            def rx(I, hp):
                pe.wait_ge(*x_ready.at(I, hp + 1))
                pe.wait_ge(*w.is_free("RX", hp))
                for t in range(NT):
                    mm = pe.transpose(psum[w.slot("RX", hp)][:, t * P:(t + 1) * P],
                                      X[hp % 2][:, t].rearrange("p i d -> p (i d)"), identf[:])
                mm.then_inc(*w.fills("RX", hp))

            def to_rows(key, tiles, cs, n_k, parts, w_h, w_l):
                for t in tiles:
                    for c in cs:
                        for k, (a_, b_) in enumerate(((parts[0], w_h), (parts[0], w_l), (parts[1], w_h))):
                            mm = pe.matmul(psum[w.slot(key)][:, t * D:(t + 1) * D], a_[:, c, t * P:(t + 1) * P], b_[:, c, :],
                                           start=(c == 0 and k == 0 and t % 2 == 0), stop=(c == n_k - 1 and k == 2),
                                           skip_group_check=True)
                return mm

            def wo_(I, c):
                pe.wait_ge(*oT_l_ready.at(I, c + 1))
                if c == 0:
                    pe.wait_ge(*w.is_free("WO"))
                mm = to_rows("WO", range(NT), (c,), NP_, (oT_h, oT_l), wo_h, wo_l)
                if c == NP_ - 1:
                    mm.then_inc(*w.fills("WO"))

            def xh_(I):
                to_columns("XH", xh, xh_ready.at(I, 1))

            def w1_(I, f):
                pe.wait_ge(*xhT_ready.at(I, 1))
                pe.wait_ge(*w.is_free("W1", f))
                for g in range(2):
                    for c in range(NC):
                        for k, (a_, b_) in enumerate(((w1_h, xhT_h), (w1_l, xhT_h), (w1_h, xhT_l))):
                            mm = pe.matmul(psum[w.slot("W1", f)][0:rows(f), g * T:(g + 1) * T], a_[:, c, hidden(g, f)], b_[:, c, :],
                                           start=(c == 0 and k == 0), stop=(c == NC - 1 and k == 2))
                mm.then_inc(*w.fills("W1", f))

            def w2_(I, part):
                if part == 0:
                    pe.wait_ge(*w.is_free("W2"))
                pe.wait_ge(*hl_ready.at(I, NF * (part + 1) // 3))
                mm = to_rows("W2", range(NT), range(NF * part // 3, NF * (part + 1) // 3), NF, (hT_h, hT_l), w2_h, w2_l)
                if part == 2:
                    mm.then_inc(*w.fills("W2"))

            with pe.Fori(0, L) as layer:
                w.run({"WB": weight_bias, "XT": xt, "QK": qk, "ST": st, "L1": l1, "LM": lm, "L2": l2, "PV": pv, "RD": rd,
                       "RX": rx, "WO": wo_, "XH": xh_, "W1": w1_, "W2": w2_}, layer)

        @block.scalar
        def _(act):
            w = Walk(ph, act, B)
            act.wait_ge(const_done, N_CONST)

            def weight_hi(I):
                K = layer_inst(w.layer)
                act.wait_ge(*w_loaded.at(K, w_loaded.per))
                act.activation(wq_h[:], st_q, ACT.Copy, scale=WSCALE).then_inc(*w_hi.up(K))
                act.activation(wo_h[:], st_o, ACT.Copy, scale=WSCALE).then_inc(*w_hi.up(K))
                act.activation(w2_h[:, 0:NF - 1, :], st_2[:, 0:NF - 1, :], ACT.Copy, scale=WSCALE)
                act.activation(w2_h[0:TAIL, NF - 1, :], st_2[0:TAIL, NF - 1, :], ACT.Copy, scale=WSCALE).then_inc(*w_hi.up(K))
                act.wait_ge(*w1_scaled.at(K, NC))
                act.activation(w1_h[:], st_1, ACT.Copy).then_inc(*w_hi.up(K))
                act.wait_ge(*w_lo.at(K, 4))
                act.wait_ge(*tables_done.at(K, 4))

            def xt(I):
                act.wait_ge(*w.is_full("XT"))
                act.activation(xT_h[:, :, 1:T + 1], psum[w.slot("XT")][:, :].rearrange("p (c t) -> p c t", c=NC), ACT.Copy)\
                    .then_inc(*xT_h_ready.up(I))

            def qk(I, t):
                act.wait_ge(*w.is_full("QK", t))
                if t > 0:
                    act.wait_ge(*q_link.at(I, RS * (t - 1) + 1))
                act.activation(sq[:], psum[w.slot("QK", t)][:, :], ACT.Square).then_inc(*sq_ready.up(I))
                act.wait_ge(*w.is_full("V", t))
                act.activation(vl[:, t, :], psum[w.slot("V", t)][:, 0:INNER], ACT.Copy, scale=1 / WSCALE).then_inc(*w.frees("V", t))

            def sh(I, t):
                r = t % 2
                act.wait_ge(*u_ready.at(I, t + 1))
                src = u[r][:].rearrange("p (i h d) -> p i h d", i=2, h=H)
                act.activation(qst[r][:, :, 0:DH], src[:, 0], ACT.Copy)
                act.activation(khh[r][:, :, :].rearrange("p h (s d) -> p h s d", s=2),
                               src[:, 1].unsqueeze(2).to_broadcast([P, H, 2, DH]), ACT.Copy).then_inc(*hi_ready.up(I))

            def st(I, t):
                act.wait_ge(*w.is_full("STa", t))
                act.activation(QT[:, :, t * P:(t + 1) * P],
                               psum[w.slot("STa", t)][:, :].bitcast(F16)[:, 0:H * P].rearrange("p (h t) -> p h t", h=H),
                               ACT.Copy).then_inc(*w.frees("STa", t))

            def lm(I):
                act.wait_ge(*w.is_full("LM"))
                act.activation(mT[0:H, :], psum[w.slot("LM")][:, :].bitcast(BF16)[0:H, 0:T], ACT.Copy).then_inc(*w.frees("LM"))

            def l2(I, h):
                act.wait_ge(*w.is_full("L2", h))
                act.activation(Pl[h % 4][:], psum[w.slot("L2", h)][:, 0:NK], ACT.Exp, scale=1 / KBOOST).then_inc(*w.frees("L2", h))

            def pv(I, hp):
                act.wait_ge(*w.is_full("PV", hp))
                act.activation(od[hp % 2][:].rearrange("p a t -> p (a t)"), psum[w.slot("PV", hp)][:, :], ACT.Copy)\
                    .then_inc(*w.frees("PV", hp))

            def ol(I, hp):
                act.wait_ge(*w.is_drained("RX", hp))
                act.activation(oT_h[:, hp, :], o[hp % 2][:], ACT.Copy).then_inc(*oT_h_ready.up(I))

            def xh_(I):
                act.wait_ge(*w.is_full("XH"))
                act.activation(xhT_h[:].rearrange("p c t -> p (c t)"), psum[w.slot("XH")][:, :], ACT.Copy).then_inc(*xhT_h_ready.up(I))

            def w1_(I, f):
                n = rows(f)
                act.wait_ge(*w.is_full("W1", f))
                act.activation(G[f % 2][0:n, :], psum[w.slot("W1", f)][0:n, T:2 * T], ACT.Gelu, bias=bias[0:n, 1, f:f + 1],
                               scale=1 / WSCALE).then_inc(*g_ready.up(I))

            def h1(I, f):
                n = rows(f)
                act.wait_ge(*w.is_drained("W1", f))
                act.activation(hT_h[0:n, f, :], hp_[f % 2][0:n, :], ACT.Copy, scale=1 / WSCALE).then_inc(*hh_ready.up(I))

            with act.Fori(0, L) as layer:
                w.run({"WB": weight_hi, "XT": xt, "QK": qk, "SH": sh, "ST": st, "LM": lm, "L2": l2, "PV": pv, "OL": ol,
                       "XH": xh_, "W1": w1_, "H1": h1}, layer)

        @block.vector
        def _(dve):
            w = Walk(ph, dve, B)
            dve.memset(mT[:], 0.0).then_inc(const_done, 1)
            dve.memset(ones[:], 1.0).then_inc(const_done, 1)
            dve.memset(zeros[:], 0.0).then_inc(const_done, 1)
            dve.memset(x1s[:].rearrange("p t d -> p (t d)"), 0.0).then_inc(const_done, 1)
            for m in (xT_h, xT_l):
                dve.memset(m[:, :, 0:2], 0.0)
            for m in (hT_h, hT_l, w2_h, w2_l):
                dve.memset(m[:, NF - 1, :], 0.0)
            dve.memset(mark_v[:], 0.0).then_inc(const_done, 1)
            dve.wait_ge(const_done, N_CONST - 2)
            dve.memset(mark_v[:], 0.0).then_inc(const_done, 2)

            def weights(I):
                K = layer_inst(w.layer)
                dve.wait_ge(*w_loaded.at(K, w_loaded.per))
                dve.wait_ge(*w.is_full("WB"))
                wb = psum[w.slot("WB")][:, 0:2 * NF].rearrange("p (g f) -> p g f", g=2)
                dve.tensor_tensor(bias[:, :, 0:NF - 1], wb[:, :, 0:NF - 1], b1_t[:, :, 0:NF - 1], ALU.add)
                dve.tensor_tensor(bias[0:TAIL, :, NF - 1], wb[0:TAIL, :, NF - 1], b1_t[0:TAIL, :, NF - 1], ALU.add)\
                    .then_inc(*w.frees("WB"))
                for c in range(NC):
                    dve.tensor_scalar(st_1[:, c, :], st_1[:, c, :], lng[:, c:c + 1], WSCALE, ALU.mult, ALU.mult)\
                        .then_inc(*w1_scaled.up(K))
                dve.wait_ge(*w1_scaled.at(K, NC))
                dve.tensor_scalar(bias[:, 0, 0:NF - 1], bias[:, 0, 0:NF - 1], WSCALE, None, ALU.mult)
                dve.tensor_scalar(bias[0:TAIL, 0, NF - 1:NF], bias[0:TAIL, 0, NF - 1:NF], WSCALE, None, ALU.mult)
                for i in range(2):
                    dve.tensor_tensor(cos_t[:, :, i, :], cos_t[:, :, i, :],
                                      qk_scale[:, i:i + 1, :].to_broadcast([P, NT, DH]), ALU.mult).then_inc(*tables_done.up(K))
                    dve.tensor_tensor(sin_t[:, :, i, :].rearrange("p t (s d) -> p t s d", s=2),
                                      sin_t[:, :, i, :].rearrange("p t (s d) -> p t s d", s=2),
                                      qk_scale[:, i, :].rearrange("p (s d) -> p s d", s=2)[:, ::-1, :].unsqueeze(1)
                                      .to_broadcast([P, NT, 2, DH // 2]), ALU.mult).then_inc(*tables_done.up(K))
                dve.wait_ge(*w_hi.at(K, 1))
                dve.scalar_tensor_tensor(wq_l[:], st_q, WSCALE, wq_h[:], ALU.mult, ALU.subtract).then_inc(*w_lo.up(K))
                dve.wait_ge(*w_hi.at(K, 2))
                dve.scalar_tensor_tensor(wo_l[:], st_o, WSCALE, wo_h[:], ALU.mult, ALU.subtract).then_inc(*w_lo.up(K))
                dve.wait_ge(*w_hi.at(K, 3))
                dve.scalar_tensor_tensor(w2_l[:, 0:NF - 1, :], st_2[:, 0:NF - 1, :], WSCALE, w2_h[:, 0:NF - 1, :],
                                         ALU.mult, ALU.subtract)
                dve.scalar_tensor_tensor(w2_l[0:TAIL, NF - 1, :], st_2[0:TAIL, NF - 1, :], WSCALE, w2_h[0:TAIL, NF - 1, :],
                                         ALU.mult, ALU.subtract).then_inc(*w_lo.up(K))
                dve.wait_ge(*w_hi.at(K, 4))
                dve.tensor_tensor(w1_l[:], st_1, w1_h[:], ALU.subtract).then_inc(*w_lo.up(K))
                dve.wait_ge(*w_lo.at(K, 4))

            def xt(I):
                dve.wait_ge(*xT_h_ready.at(I, 1))
                dve.tensor_tensor(xT_l[:, :, 1:T + 1], psum[w.slot("XT")][:, :].rearrange("p (c t) -> p c t", c=NC),
                                  xT_h[:, :, 1:T + 1], ALU.subtract).then_inc(*w.frees("XT"))
                dve.memset(mark_x[:], 0.0).then_inc(*xT_ready.up(I))

            def qk(I, t):
                def link(ins):
                    ins.then_inc(*q_link.up(I))
                    dve.wait_ge(*q_link.now(I))
                ps = psum[w.slot("QK", t)]
                dve.wait_ge(*sq_ready.at(I, t + 1))
                link(dve.tensor_reduce(ss[:], sq[:].rearrange("p (h d) -> p h d", d=DH), AX.X, ALU.add))
                link(dve.tensor_scalar(ss[:], ss[:], (NORM_MIN * WSCALE) ** 2, None, ALU.max))
                dve.tensor_tensor(u[t % 2][:].rearrange("p (i h d) -> p i h d", i=2, h=H),
                                  ps[:, :].rearrange("p (i h d) -> p i h d", i=2, h=H),
                                  cos_t[:, t, :, :].unsqueeze(2).to_broadcast([P, 2, H, DH]), ALU.mult)
                if t > 0:
                    dve.wait_ge(*bt_used.at(I, t))
                for i in range(2):
                    ins = dve.tensor_tensor(
                        bt[:, i * INNER:(i + 1) * INNER].rearrange("p (h s d) -> p h s d", h=H, s=2),
                        ps[:, i * INNER:(i + 1) * INNER].rearrange("p (h s d) -> p h s d", h=H, s=2)[:, :, ::-1, :],
                        sin_t[:, t, i, :].rearrange("p (s d) -> p s d", s=2).unsqueeze(1).to_broadcast([P, H, 2, DH // 2]),
                        ALU.mult)
                ins.then_inc(*w.frees("QK", t))
                if t > 0:
                    dve.wait_ge(*u_ready.at(I, t))
                rsqrt(dve, link, ss[:], rn[:], rt[:])

            def sh(I, t):
                r = t % 2
                src = u[r][:].rearrange("p (i h d) -> p i h d", i=2, h=H)
                dve.wait_ge(*hi_ready.at(I, t + 1))
                dve.tensor_tensor(qst[r][:, :, DH:2 * DH], src[:, 0], qst[r][:, :, 0:DH], ALU.subtract)
                dve.tensor_tensor(kll[r][:, :, 0:DH], src[:, 1], khh[r][:, :, 0:DH], ALU.subtract).then_inc(*lo_link.up(I))
                dve.wait_ge(*lo_link.now(I))
                dve.tensor_copy(kll[r][:, :, DH:2 * DH], kll[r][:, :, 0:DH]).then_inc(*stack_ready.up(I))

            def st(I, t):
                for key, dst, bank in (("STa", KH, 1), ("STb", KL, 0)):
                    dve.wait_ge(*w.is_full(key, t))
                    dve.tensor_copy(dst[:, :, t * P:(t + 1) * P],
                                    psum[w.slot(key, t)][:, :].bitcast(F16)[:, bank * H * P:(bank + 1) * H * P]
                                    .rearrange("p (h t) -> p h t", h=H)).then_inc(*w.frees(key, t))

            def l1(I, h):
                dve.wait_ge(*w.is_full("L1", h))
                dve.tensor_reduce(negm[:, :, h], psum[w.slot("L1", h)][:, :].rearrange("p (n k) -> p n k", n=NT),
                                  AX.X, ALU.max, negate=True).then_inc(*w.frees("L1", h))

            def rd(I, hp):
                dve.wait_ge(*w.is_full("RD", hp))
                dve.tensor_reduce(den[:], psum[w.slot("RD", hp)][:, 0:T].rearrange("p (t i e r) -> p t i e r", t=NT, i=2, e=2)[:, :, :, :, 0],
                                  AX.X, ALU.add).then_inc(*w.frees("RD", hp))
                dve.wait_ge(*w.is_drained("RD", hp))
                dve.reciprocal(rden[:], den[:]).then_inc(*den_link.up(I))
                dve.wait_ge(*den_link.now(I))
                dve.tensor_copy(X[hp % 2][:], rden[:].unsqueeze(3).to_broadcast([P, NT, 2, DH])).then_inc(*x_ready.up(I))

            def rx(I, hp):
                dve.wait_ge(*w.is_full("RX", hp))
                dve.tensor_tensor(o[hp % 2][:], psum[w.slot("RX", hp)][:, 0:T], od[hp % 2][:, 0, :], ALU.mult)\
                    .then_inc(*w.frees("RX", hp))

            def ol(I, hp):
                dve.wait_ge(*oT_h_ready.at(I, hp + 1))
                dve.tensor_tensor(oT_l[:, hp, :], o[hp % 2][:], oT_h[:, hp, :], ALU.subtract).then_inc(*oT_l_ready.up(I))

            def wo_(I, c):
                if c < NP_ - 1:
                    return
                dve.wait_ge(*w.is_full("WO"))
                dve.wait_ge(*xr_loaded.at(I, 16))
                dve.wait_ge(*shifted.before(I, 1))
                dve.wait_ge(*xb_ready.before(I, 1))
                dve.scalar_tensor_tensor(x1[:].rearrange("p t d -> p (t d)"), psum[w.slot("WO")][:, :], 1 / WSCALE,
                                         xr[:].rearrange("p t d -> p (t d)"), ALU.mult, ALU.add).then_inc(*w.frees("WO"))
                dve.memset(mark_v[:], 0.0).then_inc(*x1_ready.up(I))

            def ln(I):
                def link(ins):
                    ins.then_inc(*ln_link.up(I))
                    dve.wait_ge(*ln_link.now(I))
                dve.wait_ge(*xb_ready.at(I, 1))
                dve.wait_ge(*ar_loaded.at(I, 16))
                dve.scalar_tensor_tensor(xb[:].rearrange("p t d -> p (t d)"), ar[:].rearrange("p t d -> p (t d)"), is_last[:, 0:1],
                                         xb[:].rearrange("p t d -> p (t d)"), ALU.mult, ALU.add).then_inc(*z_ready.up(I))
                dve.wait_ge(*shifted.at(I, 32))
                for t in range(NT):
                    dve.bn_stats(stats[:, t, 0, :], x1[:, t, 0:D // 2])
                    ins = dve.bn_stats(stats[:, t, 1, :], x1s[:, t, :])
                link(ins)
                dve.memset(mark_v[:], 0.0)
                for t in range(NT):
                    ins = dve.bn_aggr(mv[:, t, :], stats[:, t].rearrange("p a s -> p (a s)"))
                link(ins)
                link(dve.tensor_scalar(var[:], mv[:, :, 1], EPS, None, ALU.add))
                rsqrt(dve, link, var[:], rstd[:], tmp[:])
                for t in range(NT):
                    for i, src in enumerate((x1[:, t, 0:D // 2], x1s[:, t, :])):
                        ins = dve.tensor_scalar(xh[:, t, i * (D // 2):(i + 1) * (D // 2)], src, mv[:, t, 0:1], rstd[:, t:t + 1],
                                                ALU.subtract, ALU.mult)
                ins.then_inc(*xh_ready.up(I))

            def xh_(I):
                dve.wait_ge(*xhT_h_ready.at(I, 1))
                dve.tensor_tensor(xhT_l[:].rearrange("p c t -> p (c t)"), psum[w.slot("XH")][:, :],
                                  xhT_h[:].rearrange("p c t -> p (c t)"), ALU.subtract).then_inc(*w.frees("XH"))
                dve.memset(mark_h[:], 0.0).then_inc(*xhT_ready.up(I))

            def w1_(I, f):
                n = rows(f)
                if f >= 2:
                    dve.wait_ge(*hl_ready.at(I, f - 1))
                dve.wait_ge(*g_ready.at(I, f + 1))
                dve.scalar_tensor_tensor(hp_[f % 2][0:n, :], psum[w.slot("W1", f)][0:n, 0:T], bias[0:n, 0, f:f + 1],
                                         G[f % 2][0:n, :], ALU.add, ALU.mult).then_inc(*w.frees("W1", f))

            def h1(I, f):
                n = rows(f)
                dve.wait_ge(*hh_ready.at(I, f + 1))
                dve.scalar_tensor_tensor(hT_l[0:n, f, :], hp_[f % 2][0:n, :], 1 / WSCALE, hT_h[0:n, f, :],
                                         ALU.mult, ALU.subtract).then_inc(*hl_ready.up(I))

            def w2_(I, part):
                if part < 2:
                    return
                dve.wait_ge(*w.is_full("W2"))
                dve.wait_ge(*z_ready.at(I, 1))
                dve.scalar_tensor_tensor(xb[:].rearrange("p t d -> p (t d)"), psum[w.slot("W2")][:, :], 1 / WSCALE,
                                         xb[:].rearrange("p t d -> p (t d)"), ALU.mult, ALU.add).then_inc(*w.frees("W2"))

            with dve.Fori(0, L) as layer:
                w.run({"WB": weights, "XT": xt, "QK": qk, "SH": sh, "ST": st, "L1": l1, "RD": rd, "RX": rx, "OL": ol, "WO": wo_,
                       "LN": ln, "XH": xh_, "W1": w1_, "H1": h1, "W2": w2_}, layer)

        @block.gpsimd
        def _(pool):
            w = Walk(ph, pool, B)
            mats = (ident, identb, identf, sel, masks, mask0)
            for m in mats:
                pool.memset(m[:], 0.0).then_inc(mask_zero, 1)
            pool.wait_ge(mask_zero, len(mats))
            for m in (ident, identb, identf):
                pool.affine_select(out=m[:], in_=m[:], compare_op=ALU.not_equal, fill=1.0, base=0,
                                   pattern=[[-1, P]], channel_multiplier=1).then_inc(mask_done, 1)
            pool.affine_select(out=sel[:], in_=sel[:], compare_op=ALU.not_equal, fill=1.0, base=0,
                               pattern=[[-1, H], [0, P]], channel_multiplier=1).then_inc(mask_done, 1)
            pool.affine_select(out=masks[:, 0, :], in_=masks[:, 0, :], compare_op=ALU.is_ge, fill=MASKED, base=0,
                               pattern=[[1, P]], channel_multiplier=-1).then_inc(mask_done, 1)
            pool.memset(mask0[:, 0, :], MASKED).then_inc(mask_done, 1)
            for m in (masks, mask0):
                pool.affine_select(out=m[:, 1, :], in_=m[:, 1, :], compare_op=ALU.is_ge, fill=MASKED, base=0,
                                   pattern=[[-1, P]], channel_multiplier=1).then_inc(mask_done, 1)
            pool.memset(mark_p[:], 0.0).then_inc(mask_done, 1)

            def qk(I, t):
                r = t % 2
                pool.wait_ge(*w.is_drained("QK", t))
                pool.tensor_tensor(u[r][:], u[r][:], bt[:], ALU.add).then_inc(*bt_used.up(I))
                pool.wait_ge(*bt_used.now(I))
                pool.wait_ge(*q_link.at(I, RS * (t + 1)))
                pool.tensor_tensor(u[r][:].rearrange("p (h d) -> p h d", d=DH), u[r][:].rearrange("p (h d) -> p h d", d=DH),
                                   rn[:].unsqueeze(2).to_broadcast([P, 2 * H, DH]), ALU.mult).then_inc(*u_ready.up(I))

            def ls(I):
                pool.wait_ge(*x1_ready.at(I, 1))
                pool.wait_ge(*y_stored.at(I, 0))
                pool.tensor_tensor(xb[:], x1[:], b2_t[:].unsqueeze(1).to_broadcast([P, NT, D]), ALU.add).then_inc(*xb_ready.up(I))

            with pool.Fori(0, L) as layer:
                w.run({"QK": qk, "LS": ls}, layer)

        @block.sync
        def _(sp):
            hold = lambda at: stop(sp, at, sp_held)
            w = Walk(ph, sp, B)
            ph.start_credits(sp)

            def weights(I):
                K = layer_inst(w.layer)
                layer = w.layer
                done = Inst("layer_before", 0, None)
                done.b = layer * B
                hold(y_stored.at(done, 0))
                sp.wait_ge(const_done, N_CONST)
                def load(dst, src):
                    sp.dma_start(dst, src, allow_slow_non_contiguous=True).then_inc(*w_loaded.up(K, 16))
                for c in range(NC):
                    load(st_1[:, c, :], w1[layer][c * P:(c + 1) * P, :])
                load(lnb[:], ln_b[layer].rearrange("(c p) -> p c", p=P))
                load(lng[:], ln_g[layer].rearrange("(c p) -> p c", p=P))
                for g in range(2):
                    load(b1_t[:, g, 0:NF - 1], b1[layer][g * HID:g * HID + (NF - 1) * P].rearrange("(f p) -> p f", p=P))
                    load(b1_t[0:TAIL, g, NF - 1:NF], b1[layer][g * HID + (NF - 1) * P:(g + 1) * HID].rearrange("(p o) -> p o", o=1))
                load(st_q, wqkv[layer].rearrange("(c p) n -> p c n", p=P))
                load(st_o, wo[layer].rearrange("(c p) n -> p c n", p=P))
                load(st_2[:, 0:NF - 1, :], w2[layer][0:(NF - 1) * P, :].rearrange("(f p) n -> p f n", p=P))
                load(st_2[0:TAIL, NF - 1, :], w2[layer][(NF - 1) * P:HID, :])
                load(cos_t[:], cos_d.rearrange("(t p) i d -> p t i d", p=P))
                load(sin_t[:], sin_d.rearrange("(t p) i d -> p t i d", p=P))
                load(qk_scale[:, 0, :], q_scale[layer].partition_broadcast(P))
                load(qk_scale[:, 1, :], k_scale[layer].partition_broadcast(P))
                load(b2_t[:], b2[layer].partition_broadcast(P))
                load(is_last[:], last_only_d[layer].partition_broadcast(P))

            def xt(I):
                hold(xT_ready.before(I, 1))
                sp.dma_start(xs[:], out_v[I.local]).then_inc(*x_loaded.up(I, 16))

            def xr_(I):
                hold(x1_ready.before(I, 1))
                sp.dma_start(xr[:], out_v[I.local]).then_inc(*xr_loaded.up(I, 16))

            def ls(I):
                hold(x1_ready.at(I, 1))
                hold(xh_ready.before(I, 1))
                sp.dma_start(x1s[1:P, :, :], x1[0:P - 1, :, D // 2:D]).then_inc(*shifted.up(I, 16))
                sp.dma_start(x1s[0:1, 1:NT, :], x1[P - 1:P, 0:NT - 1, D // 2:D]).then_inc(*shifted.up(I, 16))
                hold(z_ready.before(I, 1))
                sp.dma_start(ar[:], res_v[I.local]).then_inc(*ar_loaded.up(I, 16))

            def w2_(I, part):
                if part < 2:
                    return
                hold(w.is_drained("W2"))
                sp.dma_start(out_v[I.local], xb[:]).then_inc(*y_stored.up(I, 16))

            with sp.Fori(0, L) as layer:
                w.run({"WB": weights, "XT": xt, "XR": xr_, "LS": ls, "W2": w2_}, layer)
            end = Inst("after", 0, None)
            end.b = L * B
            hold(y_stored.at(end, 0))

    return ph.measured()


def program(nc, counts, x, w_qkv, w_out, wqkv, q_scale, k_scale, wo, ln_g, ln_b, w1, b1, w2, b2, out):
    attn_res = nc.dram_tensor("attn_res", x.shape, F32, kind="Internal").ap()
    found = full_attention_phase(nc, counts, x, w_qkv, w_out, out, attn_res)
    return found | layers_phase(nc, counts, wqkv, q_scale, k_scale, wo, ln_g, ln_b, w1, b1, w2, b2, out, attn_res)


_INS = ["L0_attn_x", "L0_attn_w_qkv", "L0_attn_w_out", "L0_ffn_wqkv", "L0_ffn_q_scale", "L0_ffn_k_scale", "L0_ffn_wo",
        "L0_ffn_ln_g", "L0_ffn_ln_b", "L0_ffn_w1", "L0_ffn_b1", "L0_ffn_w2", "L0_ffn_b2"]
_TRANSPOSED = ("L0_attn_w_qkv", "L0_attn_w_out")


def kernel(**inputs):
    import concourse.bacc as bacc
    from concourse.bass_utils import run_bass_kernel_spmd

    arrays = {n: np.ascontiguousarray(inputs[n].T if n in _TRANSPOSED else inputs[n]) for n in _INS}

    def build(counts):
        nc = bacc.Bacc("TRN2", target_bir_lowering=False, num_devices=1)
        args = [nc.dram_tensor("in_" + n, arrays[n].shape, mybir.dt.from_np(arrays[n].dtype), kind="ExternalInput").ap()
                for n in _INS]
        out = nc.dram_tensor("out", arrays["L0_attn_x"].shape, F32, kind="ExternalOutput").ap()
        return nc, program(nc, counts, *args, out)

    _, counts = build({})
    nc, _ = build(counts)
    r = run_bass_kernel_spmd(nc, [{"in_" + n: arrays[n] for n in _INS}], core_ids=[0])
    return r.results[0]["out"]
```

```python
from contextlib import ExitStack

import numpy as np

import concourse.bass as bass
from concourse import mybir

ALU = mybir.AluOpType
ACT = mybir.ActivationFunctionType
AX = mybir.AxisListType
F32, F16, BF16, I32 = mybir.dt.float32, mybir.dt.float16, mybir.dt.bfloat16, mybir.dt.int32

P = 128
WSCALE = 1024.0
KBOOST = 32.0
EPS = 1e-5
NORM_MIN = 1e-12
MASKED = -1e30
MAGIC = float(0x5F3759DF)


class Signal:

    def __init__(self, sem, name, per):
        self.sem, self.name, self.per, self.seen = sem, name, per, {}

    def up(self, I, n=1):
        self.seen[I.id] = self.seen.get(I.id, 0) + n
        return self.sem, n

    def at(self, I, n):
        return self.sem, I.b * self.per + (n + 1)

    def now(self, I):
        return self.at(I, self.seen[I.id])

    def before(self, I, k):
        return self.sem, (I.b - (k - 1)) * self.per + 1


class Inst:

    def __init__(self, id, par, add, first=False):
        self.id, self.par, self.add, self.first, self.b = id, par, add, first, None


class Section:
    def __init__(self, name, steps, loop=None):
        self.name, self.steps, self.loop = name, steps, loop


class PsumPlan:

    def __init__(self, pools, sections, tiles_of, outer, slow):
        slots = [s for p in pools.values() for s in p]
        self.tile, fills, frees = {}, dict.fromkeys(slots, 0), dict.fromkeys(slots, 0)
        self.per_loop = {}
        for sec in sections:
            turn = {p: {s: n - len(slots_) for n, s in enumerate(slots_)} for p, slots_ in pools.items()}
            now = 0
            open_until = dict.fromkeys(slots, -1)
            last_step = {(step[1].id, key): n for n, step in enumerate(sec.steps) for key, _, _ in tiles_of(step)}
            f0, e0 = dict(fills), dict(frees)
            for n, step in enumerate(sec.steps):
                for key, pool, n_free in tiles_of(step):
                    if n_free is None:
                        s = self.tile[(sec.name, step[1].id) + key][0]
                    else:
                        s = min((s for s in turn[pool] if open_until[s] <= n), key=turn[pool].get)
                        open_until[s] = last_step[(step[1].id, key)]
                    turn[pool][s] = now = now + 1
                    if key[0] in slow:
                        turn[pool][s] += slow[key[0]]
                    if n_free is None:
                        continue
                    self.tile[(sec.name, step[1].id) + key] = (s, fills[s], frees[s], n_free)
                    fills[s] += 1
                    frees[s] += n_free
            rounds = sec.loop[1] - sec.loop[0] if sec.loop else 1
            self.per_loop[sec.name] = {s: (fills[s] - f0[s], frees[s] - e0[s]) for s in slots}
            for s in slots:
                fills[s] = f0[s] + rounds * (fills[s] - f0[s])
                frees[s] = e0[s] + rounds * (frees[s] - e0[s])
        self.per_outer = {s: (fills[s], frees[s]) for s in slots}


def woven(order, **streams):
    found = []
    for word in order.split():
        stream, step = word.split(".")
        kind, *r = step.split(",")
        if stream in streams:
            found.append((kind, streams[stream], *[int(v) for v in r]))
    return found


class Phase:

    def __init__(self, nc, ctx, name, counts, pools, sections, tiles_of, outer=1, slow={}):
        self.nc, self.ctx, self.name, self.counts = nc, ctx, name, counts
        self.sections, self.outer = sections, outer
        self.plan = PsumPlan(pools, sections, tiles_of, outer, slow)
        self.signals = {}
        slots = [s for p in pools.values() for s in p]
        self.full = {s: ctx.enter_context(nc.semaphore(f"{name}_full_{s}")) for s in slots}
        self.free = {s: ctx.enter_context(nc.semaphore(f"{name}_free_{s}")) for s in slots}

    def new_signal(self, name):
        s = Signal(self.ctx.enter_context(self.nc.semaphore(f"{self.name}_{name}")), name,
                   self.counts.get((self.name, name), 1))
        self.signals[name] = s
        return s

    def start_credits(self, eng):
        for s in list(self.signals.values()):
            eng.sem_inc(s.sem, 1)
        for s in list(self.full.values()) + list(self.free.values()):
            eng.sem_inc(s, 1)

    def measured(self):
        out = {}
        for n, s in self.signals.items():
            seen = set(s.seen.values())
            assert len(seen) == 1, (n, s.seen)
            out[(self.name, n)] = seen.pop()
        return out


class At(tuple):

    def __new__(cls, at, count):
        self = super().__new__(cls, at)
        self.count = count
        return self


class Walk:

    def __init__(self, phase, eng, batches_per_outer=0):
        self.ph, self.eng, self.bpo = phase, eng, batches_per_outer

    def run(self, steps, layer=None):
        for sec in self.ph.sections:
            if sec.loop:
                with self.eng.Fori(sec.loop[0], sec.loop[1]) as i:
                    self.body(sec, steps, i, layer)
            else:
                self.body(sec, steps, None, layer)

    def body(self, sec, steps, i, layer):
        self.sec, self.i, self.layer = sec, i, layer
        for step in sec.steps:
            kind, I, *args = step
            if kind not in steps:
                continue
            I.b = I.add(i)
            I.local = I.b
            if layer is not None:
                I.b = I.b + layer * self.bpo
            self.I = I
            steps[kind](I, *args)

    def _count(self, s, base, which):
        v = base
        if self.sec.loop:
            v = v + (self.i - self.sec.loop[0]) * self.ph.plan.per_loop[self.sec.name][s][which]
        if self.layer is not None:
            v = v + self.layer * self.ph.plan.per_outer[s][which]
        return v

    def is_full(self, *key):
        s, fills, _, _ = self.ph.plan.tile[(self.sec.name, self.I.id) + key]
        return At((self.ph.full[s], self._count(s, fills, 0) + 2), fills)

    def is_free(self, *key):
        s, _, frees, _ = self.ph.plan.tile[(self.sec.name, self.I.id) + key]
        return At((self.ph.free[s], self._count(s, frees, 1) + 1), frees)

    def is_drained(self, *key):
        s, _, frees, n_free = self.ph.plan.tile[(self.sec.name, self.I.id) + key]
        return At((self.ph.free[s], self._count(s, frees + n_free, 1) + 1), frees + n_free)

    def wait(self, a, b):
        if a[0] is b[0]:
            self.eng.wait_ge(*max(a, b, key=lambda at: at.count))
        else:
            self.eng.wait_ge(*a)
            self.eng.wait_ge(*b)

    def fills(self, *key):
        return self.ph.full[self.slot(*key)], 1

    def frees(self, *key):
        return self.ph.free[self.slot(*key)], 1

    def slot(self, *key):
        return self.ph.plan.tile[(self.sec.name, self.I.id) + key][0]


def rsqrt(dve, link, v, y, t):
    link(dve.tensor_scalar(t.bitcast(I32), v.bitcast(I32), 1, None, ALU.logical_shift_right))
    link(dve.tensor_scalar(y.bitcast(I32), t.bitcast(I32), -1.0, MAGIC, ALU.mult, ALU.add))
    for _ in range(3):
        link(dve.tensor_tensor(t, y, y, ALU.mult))
        link(dve.scalar_tensor_tensor(t, t, -0.5, v, ALU.mult, ALU.mult))
        link(dve.scalar_tensor_tensor(y, t, 1.5, y, ALU.add, ALU.mult))


def rope_tables(T, H):
    Dh = H
    half = Dh // 2
    inv = (np.float32(1.0) / np.float32(10000.0) ** (np.arange(half, dtype=np.float32) / np.float32(half))).astype(np.float32)
    ang = (np.arange(T, dtype=np.float32)[:, None] * inv[None, :]).astype(np.float64)
    c = np.concatenate([np.cos(ang)] * 2, -1)
    s = np.concatenate([-np.sin(ang), np.sin(ang)], -1)
    sc = np.array([Dh ** -0.5, 1.0])[None, :, None] / WSCALE
    return (c[:, None, :] * sc).astype(np.float32), (s[:, None, :] * sc).astype(np.float32)


def xpos_tables(T, Dh, window, q_scale):
    f32 = np.float32
    idx = np.arange(0, Dh, 2, dtype=f32)
    inv = (f32(1.0) / f32(10000.0) ** (idx / f32(Dh))).astype(f32)
    t = np.arange(T, dtype=f32)
    ang = (t[:, None] * inv[None, :]).astype(np.float64)
    base = ((idx + f32(0.4 * Dh)) / f32(1.4 * Dh)).astype(np.float64)
    power = ((t - T // 2) / f32(window // 2)).astype(np.float64)
    scale = base[None, :] ** power[:, None]
    scale = np.concatenate([scale, scale], -1)
    c = np.concatenate([np.cos(ang)] * 2, -1)
    s = np.concatenate([-np.sin(ang), np.sin(ang)], -1)
    m = np.stack([scale * q_scale, KBOOST / scale], 1)
    return (c[:, None, :] * m).astype(f32), (s[:, None, :] * m).astype(f32)


def stop(sp, at, held):
    sp.wait_ge(*at)
    sp.sem_inc(held, 1)


def identities(pool, done, mats):
    for m in mats:
        pool.memset(m[:], 0.0).then_inc(done, 1)
    pool.wait_ge(done, len(mats))
    for m in mats:
        pool.affine_select(out=m[:], in_=m[:], compare_op=ALU.not_equal, fill=1.0, base=0,
                           pattern=[[-1, P]], channel_multiplier=1).then_inc(done, 1)


def full_attention_phase(nc, counts, x, w_qkv, w_out, out, attn_res):
    B, T, D = x.shape
    NT, NC = T // P, D // P
    H = 16
    DH = D // H
    HG = 4
    NG = H // HG
    VW = P // HG
    SW = 4 * DH + 2
    cos, sin = rope_tables(T, DH)
    cos_d = nc.inline_tensor(cos, name="rope_cos").ap()
    sin_d = nc.inline_tensor(sin, name="rope_sin").ap()

    last = B - 1
    order = """T.M2,3,0 B.M1,0 T.M2,3,1 B.M1,1 T.MV,3,0 T.MV,3,1 T.M2,3,2 B.M1,2 T.MV,3,2 T.M2,3,3 B.M1,3 T.MV,3,3 B.M1,4
               B.MM,0 T.MO,3 B.M1,5 T.MT B.M1,6 T.MP B.M2,0,0 B.M1,7 B.MV,0,0 B.M2,0,1 B.M1,8 A.LX B.MM,1 B.M2,0,2 B.MV,0,1
               A.LN,0 B.M2,0,3 B.MV,0,2 B.M1,9 B.M2,1,0 A.LN,1 B.M1,10 A.LN,2 B.MV,0,3 A.LS B.M2,1,1 B.MV,1,0 B.M1,11 B.MO,0
               A.XT B.M2,1,2 B.MV,1,1 B.M1,12 B.MM,2 A.MQ,0 B.M2,1,3 B.MV,1,2 B.M1,13 B.MV,1,3 B.M1,14 A.MQ,1 B.M2,2,0 B.MO,1
               B.M2,2,1 A.SS,0 A.MQ,2 A.SS,1 B.MV,2,0 A.MS,0 B.M1,15 A.MQ,3 B.M2,2,2 A.SS,2 A.MS,1 A.SS,3 B.MV,2,1 B.MM,3
               B.M2,2,3 A.MS,2 B.MV,2,2 B.MV,2,3 A.MS,3 B.MO,2"""
    order = " ".join(f"{w},0 {w},1" if w[2:4] in ("M1", "M2", "MV") else w for w in order.split())

    def a(name, par, add, first=False):
        return Inst(name, par, add, first)

    sections = [
        Section("start", woven(order, A=a("A_0", 0, lambda i: 0, True))),
        Section("first", woven(order, B=a("B_0", 0, lambda i: 0), A=a("A_1", 1, lambda i: 1))
                + woven(order, B=a("B_1", 1, lambda i: 1), T=a("T_0", 0, lambda i: 0), A=a("A_2", 0, lambda i: 2))),
        Section("pairs", woven(order, B=a("B_even", 0, lambda i: i * 2), T=a("T_odd", 1, lambda i: i * 2 - 1),
                               A=a("A_odd", 1, lambda i: i * 2 + 1))
                + woven(order, B=a("B_odd", 1, lambda i: i * 2 + 1), T=a("T_even", 0, lambda i: i * 2),
                        A=a("A_even", 0, lambda i: i * 2 + 2)), loop=(1, B // 2 - 1)),
        Section("end", woven(order, B=a("B_14", 0, lambda i: last - 1), T=a("T_13", 1, lambda i: last - 2),
                             A=a("A_15", 1, lambda i: last))
                + woven(order, B=a("B_15", 1, lambda i: last), T=a("T_14", 0, lambda i: last - 1))
                + woven(order, T=a("T_15", 1, lambda i: last))),
    ]
    pools = {"pair": ["p0", "p1", "p2"], "acc": ["o0", "o1"]}

    def tiles_of(step):
        kind, I, *r = step
        return {
            "XT": lambda: [(("XT",), "pair", 1)],
            "MQ": lambda: [(("MQ", *r), "pair", 2)],
            "MS": lambda: [(("MSk", *r), "pair", 1), (("MSq", *r), "pair", 1)],
            "M1": lambda: [(("M1", *r), "pair", 1)],
            "MM": lambda: [(("MM", *r), "acc", 1)],
            "M2": lambda: [(("M2", *r), "pair", 1)],
            "MV": lambda: [(("MV", r[0]), "acc", 1 if r[1] == r[2] == 0 else None)],
            "MO": lambda: [(("MO", *r), "acc", 1)],
            "MT": lambda: [(("MT",), "pair", 1)],
            "MP": lambda: [(("MP",), "pair", 1)],
        }.get(kind, lambda: [])()

    with ExitStack() as ctx:
        def sb(name, shape, dt):
            return ctx.enter_context(nc.sbuf_tensor("m_" + name, shape, dt))

        ph = Phase(nc, ctx, "m", counts, pools, sections, tiles_of)
        psum = {s: ctx.enter_context(nc.psum_tensor("m_" + s, [P, 1024], F32)) for s in pools["pair"]}
        psum |= {s: ctx.enter_context(nc.psum_tensor("m_" + s, [P, 512], F32)) for s in pools["acc"]}

        wq_h, wq_l = sb("wq_h", [P, NC, 3 * D], F16), sb("wq_l", [P, NC, 3 * D], F16)
        wo_h, wo_l = sb("wo_h", [P, NC, D], F16), sb("wo_l", [P, NC, D], F16)
        cos_t, sin_t = sb("cos", [P, NT, 2, DH], F32), sb("sin", [P, NT, 2, DH], F32)
        ident, identf = sb("ident", [P, P], F16), sb("identf", [P, P], F32)
        xin = [sb(f"xin{p}", [P, NT, D], F32) for p in range(2)]
        res, xn = sb("res", [P, NT, D], F32), sb("xn", [P, NT, D], F32)
        stats, mv = sb("stats", [P, NT, 6], F32), sb("mv", [P, NT, 2], F32)
        var, rstd, tmp = sb("var", [P, NT], F32), sb("rstd", [P, NT], F32), sb("tmp", [P, NT], F32)
        xT_h, xT_l = sb("xT_h", [P, NC, T], F16), sb("xT_l", [P, NC, T], F16)
        rc, rs = [[sb(f"{n}{r}", [P, 2 * D], F32) for r in range(2)] for n in ("rc", "rs")]
        qst, kst = [[sb(f"{n}{r}", [P, H, SW], F16) for r in range(2)] for n in ("qst", "kst")]
        QT, KT = [[sb(f"{n}{p}", [P, H, T], F16) for p in range(2)] for n in ("QT", "KT")]
        vm = [sb(f"vm{p}", [P, NT, H, VW], F32) for p in range(2)]
        negm, mT = sb("negm", [P, NT, H], F16), sb("mT", [HG, T], F16)
        Pr = [sb(f"Pr{r}", [P, HG, T], F32) for r in range(2)]
        OT = [sb(f"OT{r}", [P, T], F32) for r in range(2)]
        rden, on = sb("rden", [P, NT * HG], F32), sb("on", [P, NT, D], F32)
        oT_h, oT_l = sb("oT_h", [P, NC, T], F16), sb("oT_l", [P, NC, T], F16)
        mark_r = sb("mark_r", [1, 1], F32)
        mark_v, mark_a, mark_in = sb("mark_v", [1, 1], F32), sb("mark_a", [1, 1], F32), sb("mark_in", [1, 1], F32)
        stage_q = QT[1][:, :, :].rearrange("p h t -> p (h t)").bitcast(F32)[:, 0:NC * 3 * D].rearrange("p (c n) -> p c n", c=NC)
        stage_o = QT[1][:, :, :].rearrange("p h t -> p (h t)").bitcast(F32)[:, NC * 3 * D:NC * 4 * D].rearrange("p (c n) -> p c n", c=NC)

        res_ready = ph.new_signal("res_ready")
        x_loaded, xn_stored, res_stored = ph.new_signal("x_loaded"), ph.new_signal("xn_stored"), ph.new_signal("res_stored")
        ln_link, xn_ready = ph.new_signal("ln_link"), ph.new_signal("xn_ready")
        xT_h_ready, summed = ph.new_signal("xT_h_ready"), ph.new_signal("summed")
        split_link, stack_ready = ph.new_signal("split_link"), ph.new_signal("stack_ready")
        kv_ready, qT_ready = ph.new_signal("kv_ready"), ph.new_signal("qT_ready")
        mrow_done, oT_h_ready = ph.new_signal("mrow_done"), ph.new_signal("oT_h_ready")
        pv_done, pv_last = ph.new_signal("pv_done"), ph.new_signal("pv_last")
        rden_ready, rden_last = ph.new_signal("rden_ready"), ph.new_signal("rden_last")
        w_loaded, zeroed = [ctx.enter_context(nc.semaphore("m_" + n)) for n in ("w_loaded", "zeroed")]
        w_hi, const_done = [ctx.enter_context(nc.semaphore("m_" + n)) for n in ("w_hi", "const_done")]
        sp_held = ctx.enter_context(nc.semaphore("m_sp_held"))
        ones_done = ctx.enter_context(nc.semaphore("m_ones_done"))
        w_lo, ident_done = [ctx.enter_context(nc.semaphore("m_" + n)) for n in ("w_lo", "ident_done")]

        x_v = x.rearrange("b (t p) d -> b p t d", p=P)
        out_v = out.rearrange("b (t p) d -> b p t d", p=P)
        res_v = attn_res.rearrange("b (t p) d -> b p t d", p=P)
        block = ctx.enter_context(nc.Block())

        @block.tensor
        def _(pe):
            w = Walk(ph, pe)
            pe.wait_ge(ident_done, 4)
            pe.wait_ge(const_done, 4)
            pe.wait_ge(ones_done, 2)
            pe.wait_ge(w_lo, 2)

            def xt(I):
                pe.wait_ge(*xn_ready.at(I, NT))
                pe.wait_ge(*w.is_free("XT"))
                for c in range(NC):
                    for t in range(NT):
                        mm = pe.transpose(psum[w.slot("XT")][:, c * T + t * P:c * T + (t + 1) * P],
                                          xn[:, t, c * P:(c + 1) * P], identf[:])
                mm.then_inc(*w.fills("XT"))

            def mq(I, t):
                w.wait(w.is_drained("XT"), w.is_free("MQ", t))
                ps = psum[w.slot("MQ", t)]
                for n0, n1 in ((0, 2 * D), (2 * D, 3 * D)):
                    for c in range(NC):
                        for k, (a_, b_) in enumerate(((xT_h, wq_h), (xT_h, wq_l), (xT_l, wq_h))):
                            mm = pe.matmul(ps[:, n0:n1], a_[:, c, t * P:(t + 1) * P], b_[:, c, n0:n1],
                                           start=(c == 0 and k == 0), stop=(c == NC - 1 and k == 2))
                mm.then_inc(*w.fills("MQ", t))

            def ms(I, t):
                pe.wait_ge(*stack_ready.at(I, t + 1))
                for key, st in (("MSk", kst), ("MSq", qst)):
                    pe.wait_ge(*w.is_free(key, t))
                    ps = psum[w.slot(key, t)][:, :].bitcast(F16)
                    for h in range(H):
                        mm = pe.transpose(ps[0:4 * DH + 1, h * P:(h + 1) * P], st[t % 2][:, h, 0:4 * DH + 1], ident[:])
                    mm.then_inc(*w.fills(key, t))

            def m1(I, h, u):
                pe.wait_ge(*kv_ready.at(I, 1))
                pe.wait_ge(*qT_ready.at(I, 1))
                pe.wait_ge(*w.is_free("M1", h, u))
                for v in range(2):
                    t = 2 * u + v
                    mm = pe.matmul(psum[w.slot("M1", h, u)][:, v * T:(v + 1) * T],
                                   QT[I.par][:, h, t * P:(t + 1) * P], KT[I.par][:, h, :], start=True, stop=True)
                mm.then_inc(*w.fills("M1", h, u))

            def mmax(I, g):
                w.wait(w.is_drained("M1", (g + 1) * HG - 1, NT // 2 - 1), w.is_free("MM", g))
                ps = psum[w.slot("MM", g)][:, :].bitcast(F16)
                for t in range(NT):
                    mm = pe.transpose(ps[0:HG, t * P:(t + 1) * P], negm[:, t, g * HG:(g + 1) * HG], ident[:])
                mm.then_inc(*w.fills("MM", g))

            def m2(I, g, kt, u):
                pe.wait_ge(*mrow_done.at(I, 16 * (g + 1)))
                pe.wait_ge(*w.is_free("M2", g, kt, u))
                for v in range(2):
                    h = g * HG + 2 * u + v
                    mm = pe.matmul(psum[w.slot("M2", g, kt, u)][:, v * T:(v + 1) * T],
                                   KT[I.par][:, h, kt * P:(kt + 1) * P], QT[I.par][:, h, :], start=True, stop=True)
                mm.then_inc(*w.fills("M2", g, kt, u))

            def mv_(I, g, kt, u):
                if kt == u == 0:
                    pe.wait_ge(*w.is_free("MV", g))
                pe.wait_ge(*w.is_drained("M2", g, kt, u))
                for j in (2 * u, 2 * u + 1):
                    mm = pe.matmul(psum[w.slot("MV", g)][j * VW:(j + 1) * VW, :], vm[I.par][:, kt, g * HG + j, :],
                                   Pr[kt % 2][:, j, :], start=(kt == 0), stop=(kt == NT - 1))
                if kt == NT - 1 and u == 1:
                    mm.then_inc(*w.fills("MV", g))
                elif u == 1:
                    mm.then_inc(*(pv_last if g == NG - 1 else pv_done).up(I))

            def mo(I, g):
                w.wait(w.is_drained("MV", g), w.is_free("MO", g))
                for t in range(NT):
                    mm = pe.transpose(psum[w.slot("MO", g)][:, t * P:(t + 1) * P], OT[g % 2][:, t * P:(t + 1) * P], identf[:])
                mm.then_inc(*w.fills("MO", g))

            def mt(I):
                w.wait(w.is_drained("MO", NG - 1), w.is_free("MT"))
                for c in range(NC):
                    for t in range(NT):
                        mm = pe.transpose(psum[w.slot("MT")][:, c * T + t * P:c * T + (t + 1) * P],
                                          on[:, t, c * P:(c + 1) * P], identf[:])
                mm.then_inc(*w.fills("MT"))

            def mp(I):
                w.wait(w.is_drained("MT"), w.is_free("MP"))
                for t in range(NT):
                    for c in range(NC):
                        for k, (a_, b_) in enumerate(((oT_h, wo_h), (oT_h, wo_l), (oT_l, wo_h))):
                            mm = pe.matmul(psum[w.slot("MP")][:, t * D:(t + 1) * D], a_[:, c, t * P:(t + 1) * P],
                                           b_[:, c, :], start=(c == 0 and k == 0), stop=(c == NC - 1 and k == 2))
                mm.then_inc(*w.fills("MP"))

            w.run({"XT": xt, "MQ": mq, "MS": ms, "M1": m1, "MM": mmax, "M2": m2, "MV": mv_, "MO": mo, "MT": mt, "MP": mp})

        @block.scalar
        def _(act):
            w = Walk(ph, act)
            act.wait_ge(w_loaded, 16)
            act.activation(wq_h[:], stage_q, ACT.Copy, scale=WSCALE).then_inc(w_hi, 1)
            act.wait_ge(w_loaded, 32)
            act.activation(wo_h[:], stage_o, ACT.Copy, scale=WSCALE).then_inc(w_hi, 1)
            act.wait_ge(const_done, 4)
            act.wait_ge(ones_done, 2)
            act.wait_ge(zeroed, 5)

            def xt(I):
                act.wait_ge(*w.is_full("XT"))
                act.activation(xT_h[:].rearrange("p c t -> p (c t)"), psum[w.slot("XT")][:, :], ACT.Copy)\
                    .then_inc(*xT_h_ready.up(I))

            def mq(I, t):
                act.wait_ge(*w.is_full("MQ", t))
                act.activation(vm[I.par][:, t, :, 0:DH],
                               psum[w.slot("MQ", t)][:, 2 * D:3 * D].rearrange("p (h d) -> p h d", h=H),
                               ACT.Copy, scale=1 / WSCALE).then_inc(*w.frees("MQ", t))

            def ms(I, t):
                act.wait_ge(*w.is_full("MSk", t))
                act.activation(KT[I.par][0:4 * DH + 1, :, t * P:(t + 1) * P],
                               psum[w.slot("MSk", t)][:, :].bitcast(F16)[0:4 * DH + 1, :].rearrange("p (h t) -> p h t", h=H),
                               ACT.Copy).then_inc(*w.frees("MSk", t))
                if t == NT - 1:
                    act.activation(mark_a[:], mark_in[:], ACT.Copy).then_inc(*kv_ready.up(I))

            def mmax(I, g):
                act.wait_ge(*w.is_full("MM", g))
                act.wait_ge(*mrow_done.at(I, 16 * g))
                act.activation(mT[:], psum[w.slot("MM", g)][:, :].bitcast(F16)[0:HG, 0:T], ACT.Copy)\
                    .then_inc(*w.frees("MM", g))

            def m2(I, g, kt, u):
                n = g * NT + kt
                if u == 0 and n >= 2 and (n - 2) % NT < NT - 1:
                    g2, kt2 = divmod(n - 2, NT)
                    if g2 == NG - 1:
                        act.wait_ge(*pv_last.at(I, kt2 + 1))
                    else:
                        act.wait_ge(*pv_done.at(I, g2 * (NT - 1) + kt2 + 1))
                act.wait_ge(*w.is_full("M2", g, kt, u))
                act.activation(Pr[kt % 2][:, 2 * u:2 * u + 2, :].rearrange("p h t -> p (h t)"),
                               psum[w.slot("M2", g, kt, u)][:, :], ACT.Exp).then_inc(*w.frees("M2", g, kt, u))

            def mv_(I, g, kt, u):
                if kt < NT - 1 or u == 0:
                    return
                act.wait_ge(*w.is_full("MV", g))
                act.activation(OT[g % 2][:], psum[w.slot("MV", g)][:, :], ACT.Copy)\
                    .then_inc(*w.frees("MV", g))

            def mt(I):
                act.wait_ge(*w.is_full("MT"))
                act.activation(oT_h[:].rearrange("p c t -> p (c t)"), psum[w.slot("MT")][:, :], ACT.Copy)\
                    .then_inc(*oT_h_ready.up(I))

            w.run({"XT": xt, "MQ": mq, "MS": ms, "MM": mmax, "M2": m2, "MV": mv_, "MT": mt})

        @block.vector
        def _(dve):
            w = Walk(ph, dve)
            dve.wait_ge(w_hi, 1)
            dve.scalar_tensor_tensor(wq_l[:], stage_q, WSCALE, wq_h[:], ALU.mult, ALU.subtract).then_inc(w_lo, 1)
            dve.wait_ge(w_hi, 2)
            dve.scalar_tensor_tensor(wo_l[:], stage_o, WSCALE, wo_h[:], ALU.mult, ALU.subtract).then_inc(w_lo, 1)
            dve.wait_ge(w_lo, 2)
            for m in (QT[1], KT[1]):
                dve.memset(m[64:P, :, :].rearrange("p h t -> p (h t)").bitcast(F32), 0.0).then_inc(const_done, 1)
            dve.memset(mark_in[:], 0.0).then_inc(zeroed, 1)
            for r in range(2):
                dve.memset(qst[r][:, :, 4 * DH:SW], 0.0).then_inc(zeroed, 1)
                dve.memset(kst[r][:, :, 4 * DH:SW], 1.0).then_inc(zeroed, 1)
            dve.wait_ge(zeroed, 5)
            dve.wait_ge(w_loaded, 64)
            dve.wait_ge(const_done, 4)
            dve.wait_ge(ones_done, 2)

            def ln(I, part):
                def link(ins):
                    ins.then_inc(*ln_link.up(I))
                    dve.wait_ge(*ln_link.now(I))
                (ln_statistics, ln_rsqrt, ln_apply)[part](I, link)

            def ln_statistics(I, link):
                dve.wait_ge(*x_loaded.at(I, 16))
                for t in range(NT):
                    ins = dve.bn_stats(stats[:, t, :], xin[I.par][:, t, :])
                link(ins)
                dve.memset(mark_v[:], 0.0)
                for t in range(NT):
                    ins = dve.bn_aggr(mv[:, t, :], stats[:, t, :])
                link(ins)

            def ln_rsqrt(I, link):
                link(dve.tensor_scalar(var[:], mv[:, :, 1], EPS, None, ALU.add))
                rsqrt(dve, link, var[:], rstd[:], tmp[:])

            def ln_apply(I, link):
                if not I.first:
                    dve.wait_ge(*xn_stored.before(I, 1))
                for t in range(NT):
                    dve.tensor_scalar(xn[:, t, :], xin[I.par][:, t, :], mv[:, t, 0:1], rstd[:, t:t + 1],
                                      ALU.subtract, ALU.mult).then_inc(*xn_ready.up(I))

            def xt(I):
                dve.wait_ge(*xT_h_ready.at(I, 1))
                dve.tensor_tensor(xT_l[:].rearrange("p c t -> p (c t)"), psum[w.slot("XT")][:, :],
                                  xT_h[:].rearrange("p c t -> p (c t)"), ALU.subtract)\
                    .then_inc(*w.frees("XT"))

            def mq(I, t):
                dve.wait_ge(*w.is_full("MQ", t))
                ps = psum[w.slot("MQ", t)]
                for i in range(2):
                    dve.tensor_tensor(rc[t % 2][:, i * D:(i + 1) * D].rearrange("p (h d) -> p h d", h=H),
                                      ps[:, i * D:(i + 1) * D].rearrange("p (h d) -> p h d", h=H),
                                      cos_t[:, t, i:i + 1, :].to_broadcast([P, H, DH]), ALU.mult)
                    ins = dve.tensor_tensor(
                        rs[t % 2][:, i * D:(i + 1) * D].rearrange("p (h s d) -> p h s d", h=H, s=2),
                        ps[:, i * D:(i + 1) * D].rearrange("p (h s d) -> p h s d", h=H, s=2)[:, :, ::-1, :],
                        sin_t[:, t, i, :].rearrange("p (s d) -> p s d", s=2).unsqueeze(1).to_broadcast([P, H, 2, DH // 2]),
                        ALU.mult)
                ins.then_inc(*w.frees("MQ", t))

            def ss(I, t):
                r = t % 2
                dve.wait_ge(*summed.at(I, t + 1))
                def part(st, i):
                    return st[r][:, :, i * DH:(i + 1) * DH]
                src = rc[r][:].rearrange("p (i h d) -> p i h d", i=2, h=H)
                def two(st, i, step):
                    return st[r][:, :, 0:4 * DH].rearrange("p h (s d) -> p h s d", s=4)[:, :, i:i + step + 1:step, :]
                dve.tensor_copy(two(qst, 0, 1), src[:, 0].unsqueeze(2).to_broadcast([P, H, 2, DH])).then_inc(*split_link.up(I))
                dve.tensor_copy(two(kst, 0, 2), src[:, 1].unsqueeze(2).to_broadcast([P, H, 2, DH])).then_inc(*split_link.up(I))
                dve.wait_ge(*split_link.now(I))
                dve.tensor_tensor(part(qst, 2), src[:, 0], part(qst, 0), ALU.subtract).then_inc(*split_link.up(I))
                dve.tensor_tensor(part(kst, 1), src[:, 1], part(kst, 0), ALU.subtract).then_inc(*split_link.up(I))
                dve.wait_ge(*split_link.now(I))
                dve.tensor_copy(part(qst, 3), part(qst, 2))
                dve.tensor_copy(part(kst, 3), part(kst, 1)).then_inc(*stack_ready.up(I))

            def ms(I, t):
                dve.wait_ge(*w.is_full("MSq", t))
                dve.tensor_copy(QT[I.par][0:4 * DH + 1, :, t * P:(t + 1) * P],
                                psum[w.slot("MSq", t)][:, :].bitcast(F16)[0:4 * DH + 1, :].rearrange("p (h t) -> p h t", h=H))\
                    .then_inc(*w.frees("MSq", t))
                if t == NT - 1:
                    dve.memset(mark_v[:], 0.0).then_inc(*qT_ready.up(I))

            def m1(I, h, u):
                dve.wait_ge(*w.is_full("M1", h, u))
                dve.tensor_reduce(negm[:, 2 * u:2 * u + 2, h], psum[w.slot("M1", h, u)][:, :].rearrange("p (a k) -> p a k", a=2),
                                  AX.X, ALU.max, negate=True).then_inc(*w.frees("M1", h, u))

            def mo(I, g):
                dve.wait_ge(*w.is_full("MO", g))
                ps = psum[w.slot("MO", g)][:, 0:T].rearrange("p (a v) -> p a v", v=VW)
                ready = rden_last if g == NG - 1 else rden_ready
                dve.reciprocal(rden[:], ps[:, :, DH]).then_inc(*ready.up(I))
                dve.wait_ge(*ready.now(I))
                dve.tensor_tensor(on[:, :, g * HG * DH:(g + 1) * HG * DH].rearrange("p t (j d) -> p t j d", j=HG),
                                  ps[:, :, 0:DH].rearrange("p (t j) d -> p t j d", j=HG),
                                  rden[:].rearrange("p (t j) -> p t j", j=HG).unsqueeze(3).to_broadcast([P, NT, HG, DH]),
                                  ALU.mult).then_inc(*w.frees("MO", g))

            def mt(I):
                dve.wait_ge(*oT_h_ready.at(I, 1))
                dve.tensor_tensor(oT_l[:].rearrange("p c t -> p (c t)"), psum[w.slot("MT")][:, :],
                                  oT_h[:].rearrange("p c t -> p (c t)"), ALU.subtract)\
                    .then_inc(*w.frees("MT"))

            def mp(I):
                dve.wait_ge(*w.is_full("MP"))
                dve.wait_ge(*res_stored.at(I, 0))
                dve.scalar_tensor_tensor(res[:].rearrange("p t d -> p (t d)"), psum[w.slot("MP")][:, :], 1 / WSCALE,
                                         xin[I.par][:].rearrange("p t d -> p (t d)"), ALU.mult, ALU.add)\
                    .then_inc(*w.frees("MP"))
                dve.memset(mark_r[:], 0.0).then_inc(*res_ready.up(I))

            w.run({"LN": ln, "XT": xt, "MQ": mq, "SS": ss, "MS": ms, "M1": m1, "MO": mo, "MT": mt, "MP": mp})

        @block.gpsimd
        def _(pool):
            w = Walk(ph, pool)
            identities(pool, ident_done, (ident, identf))
            for m in vm:
                pool.memset(m[:], 1.0).then_inc(ones_done, 1)
            pool.wait_ge(ones_done, 2)
            for m in (QT[0], KT[0]):
                pool.memset(m[64:P, :, :].rearrange("p h t -> p (h t)").bitcast(F32), 0.0).then_inc(const_done, 1)

            def mq(I, t):
                pool.wait_ge(*w.is_drained("MQ", t))
                pool.tensor_tensor(rc[t % 2][:], rc[t % 2][:], rs[t % 2][:], ALU.add).then_inc(*summed.up(I))

            w.run({"MQ": mq})

        @block.sync
        def _(sp):
            hold = lambda at: stop(sp, at, sp_held)
            w = Walk(ph, sp)
            ph.start_credits(sp)
            sp.dma_start(stage_q, w_qkv.rearrange("(c p) n -> p c n", p=P)).then_inc(w_loaded, 16)
            sp.wait_ge(w_loaded, 16)
            sp.dma_start(stage_o, w_out.rearrange("(c p) n -> p c n", p=P)).then_inc(w_loaded, 16)
            sp.wait_ge(w_loaded, 32)
            sp.dma_start(cos_t[:], cos_d.rearrange("(t p) i d -> p t i d", p=P)).then_inc(w_loaded, 16)
            sp.dma_start(sin_t[:], sin_d.rearrange("(t p) i d -> p t i d", p=P)).then_inc(w_loaded, 16)

            def lx(I):
                if I.id not in ("A_0", "A_1"):
                    hold(res_ready.before(I, 2))
                sp.dma_start(xin[I.par][:], x_v[I.b]).then_inc(*x_loaded.up(I, 16))

            def ls(I):
                hold(xn_ready.at(I, NT))
                sp.dma_start(out_v[I.b], xn[:]).then_inc(*xn_stored.up(I, 16))

            def mmax(I, g):
                hold(w.is_drained("MM", g))
                sp.dma_start(QT[I.par][4 * DH:4 * DH + 1, g * HG:(g + 1) * HG, :], mT[:]).then_inc(*mrow_done.up(I, 16))

            def mp(I):
                hold(w.is_drained("MP"))
                sp.dma_start(res_v[I.b], res[:]).then_inc(*res_stored.up(I, 16))

            w.run({"LX": lx, "LS": ls, "MM": mmax, "MP": mp})
            end = Inst("after", 0, None)
            end.b = B
            hold(xn_stored.at(end, 0))
            hold(res_stored.at(end, 0))

    return ph.measured()


def layers_phase(nc, counts, wqkv, q_scale, k_scale, wo, ln_g, ln_b, w1, b1, w2, b2, out, attn_res):
    B, T, D = out.shape
    L = wqkv.shape[0]
    NT, NC = T // P, D // P
    W = P
    INNER = wo.shape[1]
    H = 8
    DH = INNER // H
    NP_ = H // 2
    HID = w2.shape[1]
    NF = -(-HID // P)
    TAIL = HID - (NF - 1) * P
    NK = 2 * (NT - 1) * W + W
    base_cos, base_sin = xpos_tables(T, DH, W, 8.0)
    cos_d = nc.inline_tensor(base_cos, name="xpos_cos").ap()
    sin_d = nc.inline_tensor(base_sin, name="xpos_sin").ap()
    last_only = np.zeros((L, 1), np.float32)
    last_only[L - 1] = 1.0
    last_only_d = nc.inline_tensor(last_only, name="last_only").ap()
    RS = 13

    order = """A.XT F.W1,0 A.QK,0 F.W1,1 A.XR F.H1,0 A.SQ,0 A.QK,1 A.HI,0 F.W1,2 A.SQ,1 A.SH,0 F.H1,1 N.LX A.QK,2 A.HI,1
               A.ST,0 F.H1,2 F.W1,3 A.SH,1 A.SQ,2 A.QK,3 A.HI,2 A.ST,1 F.H1,3 F.W1,4 A.SQ,3 F.W1,5 F.W2,0 F.W2,1 F.H1,4
               A.HI,3 A.SH,2 A.ST,2 A.SH,3 A.ST,3 F.H1,5 A.L1,0 A.L1,1 A.L1,2 A.L1,3 A.L1,4 A.L1,5 A.L1,6 A.L1,7 F.W2,2 A.LM
               N.LN A.L2,0 A.L2,1 A.L2,2 A.L2,3 A.PV,0 A.L2,4 A.RD,0 A.PV,1 A.L2,5 A.RX,0 A.L2,6 N.XH A.RD,1 N.LS A.OL,0
               A.L2,7 A.PV,2 A.RX,1 A.OL,1 A.RD,2 A.PV,3 A.RX,2 A.WO,0 N.ZB A.RD,3 A.OL,2 A.WO,1 A.RX,3 A.OL,3 A.WO,2 A.WO,3"""

    last_order = """F.W1,0 N.LX F.W1,1 F.H1,0 N.LN F.W1,2 F.H1,1 F.W1,3 F.H1,2 F.W1,4 F.H1,3 F.W1,5 F.H1,4 F.W2,0 N.XH F.H1,5
                    F.W2,1 F.W2,2 N.LS N.ZB"""

    a = lambda n, add: Inst(n, 0, add)
    prep = a("prep", lambda i: 0)
    sections = [
        Section("weights", [("WB", prep)]),
        Section("first", woven(order, A=a("A_first", lambda i: 0))),
        Section("second", woven(order, A=a("A_second", lambda i: 1), N=a("N_second", lambda i: 0))),
        Section("rounds", woven(order, A=a("A", lambda i: i), N=a("N", lambda i: i - 1), F=a("F", lambda i: i - 2)), loop=(2, B)),
        Section("last", woven(last_order, N=a("N_last", lambda i: B - 1), F=a("F_late", lambda i: B - 2))
                + woven(order, F=a("F_last", lambda i: B - 1))),
    ]
    pools = {"pair": ["p0", "p1", "p2", "p3"]}

    def tiles_of(step):
        kind, I, *r = step
        return {
            "WB": lambda: [(("WB",), "pair", 1)],
            "XT": lambda: [(("XT",), "pair", 1)],
            "QK": lambda: [(("QK", *r), "pair", 1), (("V", *r), "pair", 1)],
            "ST": lambda: [(("STa", *r), "pair", 1), (("STb", *r), "pair", 1)],
            "L1": lambda: [(("L1", *r), "pair", 1)],
            "LM": lambda: [(("LM",), "pair", 1)],
            "L2": lambda: [(("L2", *r), "pair", 1)],
            "PV": lambda: [(("PV", *r), "pair", 1)],
            "RD": lambda: [(("RD", *r), "pair", 1)],
            "RX": lambda: [(("RX", *r), "pair", 1)],
            "WO": lambda: [(("WO",), "pair", 1 if r[0] == 0 else None)],
            "XH": lambda: [(("XH",), "pair", 1)],
            "W1": lambda: [(("W1", *r), "pair", 1)],
            "W2": lambda: [(("W2",), "pair", 1 if r[0] == 0 else None)],
        }.get(kind, lambda: [])()

    with ExitStack() as ctx:
        def sb(name, shape, dt):
            return ctx.enter_context(nc.sbuf_tensor("f_" + name, shape, dt))

        ph = Phase(nc, ctx, "f", counts, pools, sections, tiles_of, outer=L, slow={"QK": 2.5})
        psum = {s: ctx.enter_context(nc.psum_tensor("f_" + s, [P, 1024], F32)) for s in pools["pair"]}

        wq_h, wq_l = sb("wq_h", [P, NC, 3 * INNER], F16), sb("wq_l", [P, NC, 3 * INNER], F16)
        wo_h, wo_l = sb("wo_h", [P, NP_, D], F16), sb("wo_l", [P, NP_, D], F16)
        w1_h, w1_l = sb("w1_h", [P, NC, 2 * HID], F16), sb("w1_l", [P, NC, 2 * HID], F16)
        w2_h, w2_l = sb("w2_h", [P, NF, D], F16), sb("w2_l", [P, NF, D], F16)
        cos_t, sin_t = sb("cos", [P, NT, 2, DH], F32), sb("sin", [P, NT, 2, DH], F32)
        qk_scale, lng, lnb = sb("qk_scale", [P, 2, DH], F32), sb("lng", [P, NC], F32), sb("lnb", [P, NC], F32)
        b1_t, bias, b2_t = sb("b1", [P, 2, NF], F32), sb("bias", [P, 2, NF], F32), sb("b2", [P, D], F32)
        is_last = sb("is_last", [P, 1], F32)
        ident, identb, identf = sb("ident", [P, P], F16), sb("identb", [P, P], BF16), sb("identf", [P, P], F32)
        masks, mask0, sel = sb("masks", [P, 2, P], BF16), sb("mask0", [P, 2, P], BF16), sb("sel", [P, H, P], BF16)
        ones = sb("ones", [P, 32], F32)
        zeros = sb("zeros", [P, P], BF16)
        xs = sb("xs", [P, NT, D], F32)
        xT_h, xT_l = sb("xT_h", [P, NC, T + 2], F16), sb("xT_l", [P, NC, T + 2], F16)
        u = [sb(f"u{r}", [P, 2 * INNER], F32) for r in range(2)]
        bt, sq = sb("bt", [P, 2 * INNER], F32), sb("sq", [P, 2 * INNER], F32)
        ss, rn, rt = sb("ss", [P, 2 * H], F32), sb("rn", [P, 2 * H], F32), sb("rt", [P, 2 * H], F32)
        qst, khh, kll = [[sb(f"{n}{r}", [P, H, 2 * DH], F16) for r in range(2)] for n in ("qst", "khh", "kll")]
        qkt = sb("qkt", [P, 3, H, T], F16)
        QT, KH, KL = qkt[:, 0], qkt[:, 1], qkt[:, 2]
        vl = sb("vl", [P, NT, INNER], F32)
        negm, mT = sb("negm", [P, NT, H], BF16), sb("mT", [P, T], BF16)
        Pl = [sb(f"Pl{r}", [P, NK], F32) for r in range(4)]
        od = [sb(f"od{r}", [P, 2, T], F32) for r in range(2)]
        den, rden = sb("den", [P, NT, 2], F32), sb("rden", [P, NT, 2], F32)
        X = [sb(f"X{r}", [P, NT, 2, DH], F32) for r in range(2)]
        o = [sb(f"o{r}", [P, T], F32) for r in range(2)]
        oT_h, oT_l = sb("oT_h", [P, NP_, T], F16), sb("oT_l", [P, NP_, T], F16)
        x1, x1s, xb = sb("x1", [P, NT, D], F32), sb("x1s", [P, NT, D // 2], F32), sb("xb", [P, NT, D], F32)
        stats, mv = sb("stats", [P, NT, 2, 6], F32), sb("mv", [P, NT, 2], F32)
        var, rstd, tmp = sb("var", [P, NT], F32), sb("rstd", [P, NT], F32), sb("tmp", [P, NT], F32)
        xh = sb("xh", [P, NT, D], F32)
        xhT_h, xhT_l = sb("xhT_h", [P, NC, T], F16), sb("xhT_l", [P, NC, T], F16)
        G, hp_ = [[sb(f"{n}{r}", [P, T], F32) for r in range(2)] for n in ("G", "hp")]
        hT_h, hT_l = sb("hT_h", [P, NF, T], F16), sb("hT_l", [P, NF, T], F16)
        ar, xr = sb("ar", [P, NT, D], F32), sb("xr", [P, NT, D], F32)
        mark_v, mark_p = sb("mark_v", [1, 1], F32), sb("mark_p", [1, 1], F32)
        mark_l = sb("mark_l", [1, H], F32)
        mark_x, mark_h = sb("mark_x", [1, 1], F32), sb("mark_h", [1, 1], F32)

        flat = qkt[:].rearrange("p a h t -> p (a h t)").bitcast(F32)
        n_q = NC * 3 * INNER
        st_q = flat[:, 0:n_q].rearrange("p (c n) -> p c n", c=NC)
        st_1 = flat[:, n_q:n_q + NC * 2 * HID].rearrange("p (c n) -> p c n", c=NC)
        st_2 = hT_h[:].rearrange("p f t -> p (f t)").bitcast(F32).rearrange("p (f n) -> p f n", f=NF)
        st_o = u[0][:].rearrange("p (f n) -> p f n", f=NP_)

        S = ph.new_signal
        wq_loaded, w1_loaded, wo_loaded, tables_loaded = S("wq_loaded"), S("w1_loaded"), S("wo_loaded"), S("tables_loaded")
        w_hi, w_lo, w1_scaled, tables_done = S("w_hi"), S("w_lo"), S("w1_scaled"), S("tables_done")
        x_loaded, xT_h_ready, sq_ready, q_link = S("x_loaded"), S("xT_h_ready"), S("sq_ready"), S("q_link")
        bt_used, u_ready, hi_ready, lo_link, stack_ready = S("bt_used"), S("u_ready"), S("hi_ready"), S("lo_link"), S("stack_ready")
        den_link, x_ready, oT_h_ready, oT_l_ready = S("den_link"), S("x_ready"), S("oT_h_ready"), S("oT_l_ready")
        x1_ready, shifted, ar_loaded, xb_ready, z_ready = S("x1_ready"), S("shifted"), S("ar_loaded"), S("xb_ready"), S("z_ready")
        ln_link, xh_ready, xhT_h_ready = S("ln_link"), S("xh_ready"), S("xhT_h_ready")
        g_ready, hh_ready, hl_ready, y_stored = S("g_ready"), S("hh_ready"), S("hl_ready"), S("y_stored")
        q_lo_ready, hs_ready, masked = S("q_lo_ready"), S("hs_ready"), S("masked")
        xT_ready, xhT_ready, xr_loaded = S("xT_ready"), S("xhT_ready"), S("xr_loaded")
        sp_held = ctx.enter_context(nc.semaphore("f_sp_held"))
        const_done, mask_zero, mask_done = [ctx.enter_context(nc.semaphore("f_" + n)) for n in ("const_done", "mask_zero", "mask_done")]
        N_CONST, N_MASK = 7, 9

        out_v = out.rearrange("b (t p) d -> b p t d", p=P)
        res_v = attn_res.rearrange("b (t p) d -> b p t d", p=P)
        block = ctx.enter_context(nc.Block())

        def layer_inst(layer):
            I = Inst("layer", 0, None)
            I.b = layer
            return I

        def rows(f):
            return P if f < NF - 1 else TAIL

        def hidden(g, f):
            return slice(g * HID + f * P, g * HID + f * P + rows(f))

        @block.tensor
        def _(pe):
            w = Walk(ph, pe, B)
            pe.wait_ge(const_done, N_CONST)
            pe.wait_ge(mask_done, N_MASK)

            def weight_bias(I):
                K = layer_inst(w.layer)
                pe.wait_ge(*w1_loaded.at(K, w1_loaded.per))
                pe.wait_ge(*w.is_free("WB"))
                for g in range(2):
                    for f in range(NF):
                        for c in range(NC):
                            mm = pe.matmul(psum[w.slot("WB")][0:rows(f), g * NF + f:g * NF + f + 1],
                                           st_1[:, c, hidden(g, f)], lnb[:, c:c + 1], start=(c == 0), stop=(c == NC - 1))
                mm.then_inc(*w.fills("WB"))
                pe.wait_ge(*w_lo.at(K, 4))
                pe.wait_ge(*tables_done.at(K, 4))

            def to_columns(key, src, ready):
                pe.wait_ge(*ready)
                pe.wait_ge(*w.is_free(key))
                for c in range(NC):
                    for t in range(NT):
                        mm = pe.transpose(psum[w.slot(key)][:, c * T + t * P:c * T + (t + 1) * P],
                                          src[:, t, c * P:(c + 1) * P], identf[:])
                mm.then_inc(*w.fills(key))

            def xt(I):
                to_columns("XT", xs, x_loaded.at(I, 16))

            def qk(I, t):
                pe.wait_ge(*xT_ready.at(I, 1))
                for key, cols in (("QK", (0, INNER)), ("V", (2 * INNER,))):
                    pe.wait_ge(*w.is_free(key, t))
                    for i, n0 in enumerate(cols):
                        for c in range(NC):
                            at = slice(t * P + 1 - c, (t + 1) * P + 1 - c)
                            for k, (a_, b_) in enumerate(((xT_h, wq_h), (xT_h, wq_l), (xT_l, wq_h))):
                                mm = pe.matmul(psum[w.slot(key, t)][:, i * INNER:(i + 1) * INNER], a_[:, c, at],
                                               b_[:, c, n0:n0 + INNER], start=(c == 0 and k == 0), stop=(c == NC - 1 and k == 2))
                    mm.then_inc(*w.fills(key, t))

            def st(I, t):
                r = t % 2
                for key, ready, parts in (("STa", q_lo_ready, (qst, khh)), ("STb", stack_ready, (kll,))):
                    pe.wait_ge(*ready.at(I, t + 1))
                    pe.wait_ge(*w.is_free(key, t))
                    ps = psum[w.slot(key, t)][:, :].bitcast(F16)
                    for i, m in enumerate(parts):
                        for h in range(H):
                            mm = pe.transpose(ps[:, (i * H + h) * P:(i * H + h + 1) * P], m[r][:, h, :], ident[:])
                    mm.then_inc(*w.fills(key, t))

            def l1(I, h):
                w.wait(w.is_drained("STa", NT - 1), w.is_free("L1", h))
                ps = psum[w.slot("L1", h)]
                for n in range(NT):
                    lo = 1 if n == 0 else 0
                    pe.matmul(ps[:, 2 * n * W:2 * (n + 1) * W], identb[:], (mask0 if n == 0 else masks)[:].rearrange("p a k -> p (a k)"),
                              start=True, stop=False, skip_group_check=True)
                    mm = pe.matmul(ps[:, (2 * n + lo) * W:2 * (n + 1) * W], QT[:, h, n * W:(n + 1) * W],
                                   KH[:, h, (n - 1 + lo) * W:(n + 1) * W], start=False, stop=True, skip_group_check=True)
                mm.then_inc(*w.fills("L1", h))

            def lm(I):
                w.wait(w.is_drained("L1", H - 1), w.is_free("LM"))
                ps = psum[w.slot("LM")][:, :].bitcast(BF16)
                for t in range(NT):
                    mm = pe.transpose(ps[0:H, t * P:(t + 1) * P], negm[:, t, :], identb[:])
                mm.then_inc(*w.fills("LM"))

            def l2(I, h):
                w.wait(w.is_drained("LM"), w.is_free("L2", h))
                ps = psum[w.slot("L2", h)]
                for j in range(NT):
                    n = min(2 * W, T - j * W)
                    dst = ps[:, 2 * j * W:2 * j * W + n]
                    q = slice(j * W, j * W + n)
                    pe.matmul(dst, sel[:, h, :], mT[:, q], start=True, stop=False, skip_group_check=True)
                    pe.matmul(dst, KH[:, h, j * W:(j + 1) * W], QT[:, h, q], start=False, stop=False, skip_group_check=True)
                    mm = pe.matmul(dst, KL[:, h, j * W:(j + 1) * W], QT[:, h, q], start=False, stop=True, skip_group_check=True)
                mm.then_inc(*w.fills("L2", h))

            def pv(I, hp):
                pe.wait_ge(*masked.at(I, 2 * (2 * hp + 2)))
                pe.wait_ge(*w.is_free("PV", hp))
                ps = psum[w.slot("PV", hp)]
                for j in range(NT):
                    n = min(2 * W, T - j * W)
                    for i in range(2):
                        h = 2 * hp + i
                        pe.matmul(ps[i * DH:(i + 1) * DH, j * W:j * W + n], vl[:, j, h * DH:(h + 1) * DH],
                                  Pl[h % 4][:, 2 * j * W:2 * j * W + n], start=(j == 0), stop=(j == NT - 1), skip_group_check=True)
                for i in range(2):
                    pe.matmul(ps[i * DH + 32:i * DH + 64, T:T + W], zeros[:, 0:32], zeros[:, :], start=True, stop=False,
                              skip_group_check=True)
                for j0 in range(0, NT, 2):
                    for i in range(2):
                        for j in (j0, j0 + 1):
                            n = min(2 * W, T - j * W)
                            r0 = i * DH + 32 * (j % 2)
                            mm = pe.matmul(ps[r0:r0 + 32, T + j * W:T + j * W + n], ones[:],
                                           Pl[(2 * hp + i) % 4][:, 2 * j * W:2 * j * W + n], start=(j == 0), stop=(j >= NT - 2),
                                           skip_group_check=True)
                mm.then_inc(*w.fills("PV", hp))

            def rd(I, hp):
                w.wait(w.is_drained("PV", hp), w.is_free("RD", hp))
                for t in range(NT):
                    mm = pe.transpose(psum[w.slot("RD", hp)][:, t * P:(t + 1) * P], od[hp % 2][:, 1, t * P:(t + 1) * P], identf[:])
                mm.then_inc(*w.fills("RD", hp))

            def rx(I, hp):
                pe.wait_ge(*x_ready.at(I, hp + 1))
                pe.wait_ge(*w.is_free("RX", hp))
                for t in range(NT):
                    mm = pe.transpose(psum[w.slot("RX", hp)][:, t * P:(t + 1) * P],
                                      X[hp % 2][:, t].rearrange("p i d -> p (i d)"), identf[:])
                mm.then_inc(*w.fills("RX", hp))

            def to_rows(key, tiles, cs, n_k, parts, w_h, w_l):
                for t in tiles:
                    for c in cs:
                        for k, (a_, b_) in enumerate(((parts[0], w_h), (parts[0], w_l), (parts[1], w_h))):
                            mm = pe.matmul(psum[w.slot(key)][:, t * D:(t + 1) * D], a_[:, c, t * P:(t + 1) * P], b_[:, c, :],
                                           start=(c == 0 and k == 0 and t % 2 == 0), stop=(c == n_k - 1 and k == 2),
                                           skip_group_check=True)
                return mm

            def wo_(I, c):
                pe.wait_ge(*oT_l_ready.at(I, c + 1))
                if c == 0:
                    pe.wait_ge(*w.is_free("WO"))
                mm = to_rows("WO", range(NT), (c,), NP_, (oT_h, oT_l), wo_h, wo_l)
                if c == NP_ - 1:
                    mm.then_inc(*w.fills("WO"))

            def xh_(I):
                to_columns("XH", xh, xh_ready.at(I, 1))

            def w1_(I, f):
                pe.wait_ge(*xhT_ready.at(I, 1))
                pe.wait_ge(*w.is_free("W1", f))
                for g in range(2):
                    for c in range(NC):
                        for k, (a_, b_) in enumerate(((w1_h, xhT_h), (w1_l, xhT_h), (w1_h, xhT_l))):
                            mm = pe.matmul(psum[w.slot("W1", f)][0:rows(f), g * T:(g + 1) * T], a_[:, c, hidden(g, f)], b_[:, c, :],
                                           start=(c == 0 and k == 0), stop=(c == NC - 1 and k == 2))
                mm.then_inc(*w.fills("W1", f))

            def w2_(I, part):
                if part == 0:
                    pe.wait_ge(*w.is_free("W2"))
                pe.wait_ge(*hl_ready.at(I, NF * (part + 1) // 3))
                mm = to_rows("W2", range(NT), range(NF * part // 3, NF * (part + 1) // 3), NF, (hT_h, hT_l), w2_h, w2_l)
                if part == 2:
                    mm.then_inc(*w.fills("W2"))

            with pe.Fori(0, L) as layer:
                w.run({"WB": weight_bias, "XT": xt, "QK": qk, "ST": st, "L1": l1, "LM": lm, "L2": l2, "PV": pv, "RD": rd,
                       "RX": rx, "WO": wo_, "XH": xh_, "W1": w1_, "W2": w2_}, layer)

        @block.scalar
        def _(act):
            w = Walk(ph, act, B)
            act.wait_ge(const_done, N_CONST)

            def weight_hi(I):
                K = layer_inst(w.layer)
                act.wait_ge(*wq_loaded.at(K, wq_loaded.per))
                act.activation(wq_h[:], st_q, ACT.Copy, scale=WSCALE).then_inc(*w_hi.up(K))
                act.wait_ge(*wo_loaded.at(K, wo_loaded.per))
                act.activation(wo_h[:], st_o, ACT.Copy, scale=WSCALE).then_inc(*w_hi.up(K))
                act.activation(w2_h[:, 0:NF - 1, :], st_2[:, 0:NF - 1, :], ACT.Copy, scale=WSCALE)
                act.activation(w2_h[0:TAIL, NF - 1, :], st_2[0:TAIL, NF - 1, :], ACT.Copy, scale=WSCALE).then_inc(*w_hi.up(K))
                act.wait_ge(*w1_scaled.at(K, NC))
                act.activation(w1_h[:], st_1, ACT.Copy).then_inc(*w_hi.up(K))
                act.wait_ge(*w_lo.at(K, 4))
                act.wait_ge(*tables_done.at(K, 4))

            def xt(I):
                act.wait_ge(*w.is_full("XT"))
                act.activation(xT_h[:, :, 1:T + 1], psum[w.slot("XT")][:, :].rearrange("p (c t) -> p c t", c=NC), ACT.Copy)\
                    .then_inc(*xT_h_ready.up(I))

            def qk(I, t):
                act.wait_ge(*w.is_full("QK", t))
                if t > 0:
                    act.wait_ge(*q_link.at(I, RS * (t - 1) + 1))
                act.activation(sq[:], psum[w.slot("QK", t)][:, :], ACT.Square).then_inc(*sq_ready.up(I))
                act.wait_ge(*w.is_full("V", t))
                act.activation(vl[:, t, :], psum[w.slot("V", t)][:, 0:INNER], ACT.Copy, scale=1 / WSCALE).then_inc(*w.frees("V", t))

            def hi(I, t):
                r = t % 2
                act.wait_ge(*u_ready.at(I, t + 1))
                src = u[r][:].rearrange("p (i h d) -> p i h d", i=2, h=H)
                act.activation(qst[r][:, :, 0:DH], src[:, 0], ACT.Copy)
                act.activation(khh[r][:, :, :].rearrange("p h (s d) -> p h s d", s=2),
                               src[:, 1].unsqueeze(2).to_broadcast([P, H, 2, DH]), ACT.Copy).then_inc(*hi_ready.up(I))

            def st(I, t):
                act.wait_ge(*w.is_full("STa", t))
                act.activation(qkt[:, 0:2, :, t * P:(t + 1) * P],
                               psum[w.slot("STa", t)][:, :].bitcast(F16).rearrange("p (a h t) -> p a h t", a=2, h=H),
                               ACT.Copy).then_inc(*w.frees("STa", t))
                act.wait_ge(*w.is_full("STb", t))
                act.activation(KL[:, :, t * P:(t + 1) * P],
                               psum[w.slot("STb", t)][:, :].bitcast(F16)[:, 0:H * P].rearrange("p (h t) -> p h t", h=H),
                               ACT.Copy).then_inc(*w.frees("STb", t))

            def lm(I):
                act.wait_ge(*w.is_full("LM"))
                act.activation(mT[0:H, :], psum[w.slot("LM")][:, :].bitcast(BF16)[0:H, 0:T], ACT.Copy).then_inc(*w.frees("LM"))

            def l2(I, h):
                act.wait_ge(*w.is_full("L2", h))
                act.activation(Pl[h % 4][:], psum[w.slot("L2", h)][:, 0:NK], ACT.Exp, scale=1 / KBOOST).then_inc(*w.frees("L2", h))

            def pv(I, hp):
                act.wait_ge(*w.is_full("PV", hp))
                act.activation(od[hp % 2][:].rearrange("p a t -> p (a t)"), psum[w.slot("PV", hp)][:, :], ACT.Copy)\
                    .then_inc(*w.frees("PV", hp))

            def ol(I, hp):
                act.wait_ge(*w.is_drained("RX", hp))
                act.activation(oT_h[:, hp, :], o[hp % 2][:], ACT.Copy).then_inc(*oT_h_ready.up(I))

            def xh_(I):
                act.wait_ge(*w.is_full("XH"))
                act.activation(xhT_h[:].rearrange("p c t -> p (c t)"), psum[w.slot("XH")][:, :], ACT.Copy).then_inc(*xhT_h_ready.up(I))

            def w1_(I, f):
                n = rows(f)
                act.wait_ge(*w.is_full("W1", f))
                act.activation(G[f % 2][0:n, :], psum[w.slot("W1", f)][0:n, T:2 * T], ACT.Gelu, bias=bias[0:n, 1, f:f + 1],
                               scale=1 / WSCALE).then_inc(*g_ready.up(I))

            def h1(I, f):
                n = rows(f)
                act.wait_ge(*w.is_drained("W1", f))
                act.activation(hT_h[0:n, f, :], hp_[f % 2][0:n, :], ACT.Copy, scale=1 / WSCALE).then_inc(*hh_ready.up(I))
                act.wait_ge(*hh_ready.now(I))
                act.activation(hp_[f % 2][0:n, :], hp_[f % 2][0:n, :], ACT.Copy, scale=1 / WSCALE).then_inc(*hs_ready.up(I))

            with act.Fori(0, L) as layer:
                w.run({"WB": weight_hi, "XT": xt, "QK": qk, "HI": hi, "ST": st, "LM": lm, "L2": l2, "PV": pv, "OL": ol,
                       "XH": xh_, "W1": w1_, "H1": h1}, layer)

        @block.vector
        def _(dve):
            w = Walk(ph, dve, B)
            dve.memset(mT[:], 0.0).then_inc(const_done, 1)
            dve.memset(ones[:], 1.0).then_inc(const_done, 1)
            dve.memset(zeros[:], 0.0).then_inc(const_done, 1)
            dve.memset(x1s[:].rearrange("p t d -> p (t d)"), 0.0).then_inc(const_done, 1)
            for m in (xT_h, xT_l):
                dve.memset(m[:, :, 0:2], 0.0)
            for m in (hT_h, hT_l, w2_h, w2_l):
                dve.memset(m[:, NF - 1, :], 0.0)
            dve.memset(mark_v[:], 0.0).then_inc(const_done, 1)
            dve.wait_ge(const_done, N_CONST - 2)
            dve.memset(mark_v[:], 0.0).then_inc(const_done, 2)

            def weights(I):
                K = layer_inst(w.layer)
                dve.wait_ge(*w_hi.at(K, 1))
                dve.scalar_tensor_tensor(wq_l[:], st_q, WSCALE, wq_h[:], ALU.mult, ALU.subtract).then_inc(*w_lo.up(K))
                dve.wait_ge(*w_hi.at(K, 2))
                dve.scalar_tensor_tensor(wo_l[:], st_o, WSCALE, wo_h[:], ALU.mult, ALU.subtract).then_inc(*w_lo.up(K))
                dve.wait_ge(*w_hi.at(K, 3))
                dve.scalar_tensor_tensor(w2_l[:, 0:NF - 1, :], st_2[:, 0:NF - 1, :], WSCALE, w2_h[:, 0:NF - 1, :],
                                         ALU.mult, ALU.subtract)
                dve.scalar_tensor_tensor(w2_l[0:TAIL, NF - 1, :], st_2[0:TAIL, NF - 1, :], WSCALE, w2_h[0:TAIL, NF - 1, :],
                                         ALU.mult, ALU.subtract).then_inc(*w_lo.up(K))
                dve.wait_ge(*tables_loaded.at(K, tables_loaded.per))
                for i in range(2):
                    dve.tensor_tensor(cos_t[:, :, i, :], cos_t[:, :, i, :],
                                      qk_scale[:, i:i + 1, :].to_broadcast([P, NT, DH]), ALU.mult).then_inc(*tables_done.up(K))
                    dve.tensor_tensor(sin_t[:, :, i, :].rearrange("p t (s d) -> p t s d", s=2),
                                      sin_t[:, :, i, :].rearrange("p t (s d) -> p t s d", s=2),
                                      qk_scale[:, i, :].rearrange("p (s d) -> p s d", s=2)[:, ::-1, :].unsqueeze(1)
                                      .to_broadcast([P, NT, 2, DH // 2]), ALU.mult).then_inc(*tables_done.up(K))
                dve.wait_ge(*w1_loaded.at(K, w1_loaded.per))
                dve.wait_ge(*w.is_full("WB"))
                wb = psum[w.slot("WB")][:, 0:2 * NF].rearrange("p (g f) -> p g f", g=2)
                dve.tensor_tensor(bias[:, :, 0:NF - 1], wb[:, :, 0:NF - 1], b1_t[:, :, 0:NF - 1], ALU.add)
                dve.tensor_tensor(bias[0:TAIL, :, NF - 1], wb[0:TAIL, :, NF - 1], b1_t[0:TAIL, :, NF - 1], ALU.add)\
                    .then_inc(*w.frees("WB"))
                for c in range(NC):
                    dve.tensor_scalar(st_1[:, c, :], st_1[:, c, :], lng[:, c:c + 1], WSCALE, ALU.mult, ALU.mult)\
                        .then_inc(*w1_scaled.up(K))
                dve.wait_ge(*w1_scaled.at(K, NC))
                dve.tensor_scalar(bias[:, 0, 0:NF - 1], bias[:, 0, 0:NF - 1], WSCALE, None, ALU.mult)
                dve.tensor_scalar(bias[0:TAIL, 0, NF - 1:NF], bias[0:TAIL, 0, NF - 1:NF], WSCALE, None, ALU.mult)
                dve.wait_ge(*w_hi.at(K, 4))
                dve.tensor_tensor(w1_l[:], st_1, w1_h[:], ALU.subtract).then_inc(*w_lo.up(K))
                dve.wait_ge(*w_lo.at(K, 4))

            def xt(I):
                dve.wait_ge(*xT_h_ready.at(I, 1))
                dve.tensor_tensor(xT_l[:, :, 1:T + 1], psum[w.slot("XT")][:, :].rearrange("p (c t) -> p c t", c=NC),
                                  xT_h[:, :, 1:T + 1], ALU.subtract).then_inc(*w.frees("XT"))
                dve.memset(mark_x[:], 0.0).then_inc(*xT_ready.up(I))

            def qk(I, t):
                def link(ins):
                    ins.then_inc(*q_link.up(I))
                    dve.wait_ge(*q_link.now(I))
                ps = psum[w.slot("QK", t)]
                dve.wait_ge(*sq_ready.at(I, t + 1))
                link(dve.tensor_reduce(ss[:], sq[:].rearrange("p (h d) -> p h d", d=DH), AX.X, ALU.add))
                link(dve.tensor_scalar(ss[:], ss[:], (NORM_MIN * WSCALE) ** 2, None, ALU.max))
                if t >= 2:
                    dve.wait_ge(*q_lo_ready.at(I, t - 1))
                dve.tensor_tensor(u[t % 2][:].rearrange("p (i h d) -> p i h d", i=2, h=H),
                                  ps[:, :].rearrange("p (i h d) -> p i h d", i=2, h=H),
                                  cos_t[:, t, :, :].unsqueeze(2).to_broadcast([P, 2, H, DH]), ALU.mult)
                if t > 0:
                    dve.wait_ge(*bt_used.at(I, t))
                for i in range(2):
                    ins = dve.tensor_tensor(
                        bt[:, i * INNER:(i + 1) * INNER].rearrange("p (h s d) -> p h s d", h=H, s=2),
                        ps[:, i * INNER:(i + 1) * INNER].rearrange("p (h s d) -> p h s d", h=H, s=2)[:, :, ::-1, :],
                        sin_t[:, t, i, :].rearrange("p (s d) -> p s d", s=2).unsqueeze(1).to_broadcast([P, H, 2, DH // 2]),
                        ALU.mult)
                ins.then_inc(*w.frees("QK", t))
                if t > 0:
                    dve.wait_ge(*u_ready.at(I, t))
                rsqrt(dve, link, ss[:], rn[:], rt[:])

            def sh(I, t):
                r = t % 2
                src = u[r][:].rearrange("p (i h d) -> p i h d", i=2, h=H)
                dve.wait_ge(*hi_ready.at(I, t + 1))
                dve.tensor_tensor(kll[r][:, :, 0:DH], src[:, 1], khh[r][:, :, 0:DH], ALU.subtract).then_inc(*lo_link.up(I))
                dve.wait_ge(*lo_link.now(I))
                dve.tensor_copy(kll[r][:, :, DH:2 * DH], kll[r][:, :, 0:DH]).then_inc(*stack_ready.up(I))

            def l1(I, h):
                dve.wait_ge(*w.is_full("L1", h))
                dve.tensor_reduce(negm[:, :, h], psum[w.slot("L1", h)][:, :].rearrange("p (n k) -> p n k", n=NT),
                                  AX.X, ALU.max, negate=True).then_inc(*w.frees("L1", h))

            def rd(I, hp):
                dve.wait_ge(*w.is_full("RD", hp))
                dve.tensor_reduce(den[:], psum[w.slot("RD", hp)][:, 0:T].rearrange("p (t i e r) -> p t i e r", t=NT, i=2, e=2)[:, :, :, :, 0],
                                  AX.X, ALU.add).then_inc(*w.frees("RD", hp))
                dve.wait_ge(*w.is_drained("RD", hp))
                dve.reciprocal(rden[:], den[:]).then_inc(*den_link.up(I))
                dve.wait_ge(*den_link.now(I))
                dve.tensor_copy(X[hp % 2][:], rden[:].unsqueeze(3).to_broadcast([P, NT, 2, DH])).then_inc(*x_ready.up(I))

            def rx(I, hp):
                dve.wait_ge(*w.is_full("RX", hp))
                dve.tensor_tensor(o[hp % 2][:], psum[w.slot("RX", hp)][:, 0:T], od[hp % 2][:, 0, :], ALU.mult)\
                    .then_inc(*w.frees("RX", hp))

            def ol(I, hp):
                dve.wait_ge(*oT_h_ready.at(I, hp + 1))
                dve.tensor_tensor(oT_l[:, hp, :], o[hp % 2][:], oT_h[:, hp, :], ALU.subtract).then_inc(*oT_l_ready.up(I))

            def wo_(I, c):
                if c < NP_ - 1:
                    return
                dve.wait_ge(*w.is_full("WO"))
                dve.wait_ge(*xr_loaded.at(I, 16))
                dve.wait_ge(*shifted.before(I, 1))
                dve.wait_ge(*xb_ready.before(I, 1))
                dve.scalar_tensor_tensor(x1[:].rearrange("p t d -> p (t d)"), psum[w.slot("WO")][:, :], 1 / WSCALE,
                                         xr[:].rearrange("p t d -> p (t d)"), ALU.mult, ALU.add).then_inc(*w.frees("WO"))
                dve.memset(mark_v[:], 0.0).then_inc(*x1_ready.up(I))

            def zb(I):
                dve.wait_ge(*xb_ready.at(I, 1))
                dve.wait_ge(*ar_loaded.at(I, 16))
                dve.scalar_tensor_tensor(xb[:].rearrange("p t d -> p (t d)"), ar[:].rearrange("p t d -> p (t d)"), is_last[:, 0:1],
                                         xb[:].rearrange("p t d -> p (t d)"), ALU.mult, ALU.add).then_inc(*z_ready.up(I))

            def ln(I):
                def link(ins):
                    ins.then_inc(*ln_link.up(I))
                    dve.wait_ge(*ln_link.now(I))
                dve.wait_ge(*shifted.at(I, 32))
                for t in range(NT):
                    dve.bn_stats(stats[:, t, 0, :], x1[:, t, 0:D // 2])
                    ins = dve.bn_stats(stats[:, t, 1, :], x1s[:, t, :])
                link(ins)
                dve.memset(mark_v[:], 0.0)
                for t in range(NT):
                    ins = dve.bn_aggr(mv[:, t, :], stats[:, t].rearrange("p a s -> p (a s)"))
                link(ins)
                link(dve.tensor_scalar(var[:], mv[:, :, 1], EPS, None, ALU.add))
                rsqrt(dve, link, var[:], rstd[:], tmp[:])
                for t in range(NT):
                    for i, src in enumerate((x1[:, t, 0:D // 2], x1s[:, t, :])):
                        ins = dve.tensor_scalar(xh[:, t, i * (D // 2):(i + 1) * (D // 2)], src, mv[:, t, 0:1], rstd[:, t:t + 1],
                                                ALU.subtract, ALU.mult)
                ins.then_inc(*xh_ready.up(I))

            def xh_(I):
                dve.wait_ge(*xhT_h_ready.at(I, 1))
                dve.tensor_tensor(xhT_l[:].rearrange("p c t -> p (c t)"), psum[w.slot("XH")][:, :],
                                  xhT_h[:].rearrange("p c t -> p (c t)"), ALU.subtract).then_inc(*w.frees("XH"))
                dve.memset(mark_h[:], 0.0).then_inc(*xhT_ready.up(I))

            def w1_(I, f):
                n = rows(f)
                if f >= 2:
                    dve.wait_ge(*hl_ready.at(I, f - 1))
                dve.wait_ge(*g_ready.at(I, f + 1))
                dve.scalar_tensor_tensor(hp_[f % 2][0:n, :], psum[w.slot("W1", f)][0:n, 0:T], bias[0:n, 0, f:f + 1],
                                         G[f % 2][0:n, :], ALU.add, ALU.mult).then_inc(*w.frees("W1", f))

            def w2_(I, part):
                if part < 2:
                    return
                dve.wait_ge(*w.is_full("W2"))
                dve.wait_ge(*z_ready.at(I, 1))
                dve.scalar_tensor_tensor(xb[:].rearrange("p t d -> p (t d)"), psum[w.slot("W2")][:, :], 1 / WSCALE,
                                         xb[:].rearrange("p t d -> p (t d)"), ALU.mult, ALU.add).then_inc(*w.frees("W2"))

            with dve.Fori(0, L) as layer:
                w.run({"WB": weights, "XT": xt, "QK": qk, "SH": sh, "L1": l1, "RD": rd, "RX": rx, "OL": ol, "WO": wo_,
                       "LN": ln, "ZB": zb, "XH": xh_, "W1": w1_, "W2": w2_}, layer)

        @block.gpsimd
        def _(pool):
            w = Walk(ph, pool, B)
            mats = (ident, identb, identf, sel, masks, mask0)
            for m in mats:
                pool.memset(m[:], 0.0).then_inc(mask_zero, 1)
            pool.wait_ge(mask_zero, len(mats))
            for m in (ident, identb, identf):
                pool.affine_select(out=m[:], in_=m[:], compare_op=ALU.not_equal, fill=1.0, base=0,
                                   pattern=[[-1, P]], channel_multiplier=1).then_inc(mask_done, 1)
            pool.affine_select(out=sel[:], in_=sel[:], compare_op=ALU.not_equal, fill=1.0, base=0,
                               pattern=[[-1, H], [0, P]], channel_multiplier=1).then_inc(mask_done, 1)
            pool.affine_select(out=masks[:, 0, :], in_=masks[:, 0, :], compare_op=ALU.is_ge, fill=MASKED, base=0,
                               pattern=[[1, P]], channel_multiplier=-1).then_inc(mask_done, 1)
            pool.memset(mask0[:, 0, :], MASKED).then_inc(mask_done, 1)
            for m in (masks, mask0):
                pool.affine_select(out=m[:, 1, :], in_=m[:, 1, :], compare_op=ALU.is_ge, fill=MASKED, base=0,
                                   pattern=[[-1, P]], channel_multiplier=1).then_inc(mask_done, 1)
            pool.memset(mark_p[:], 0.0).then_inc(mask_done, 1)

            def qk(I, t):
                r = t % 2
                pool.wait_ge(*w.is_drained("QK", t))
                pool.tensor_tensor(u[r][:], u[r][:], bt[:], ALU.add).then_inc(*bt_used.up(I))
                pool.wait_ge(*bt_used.now(I))
                pool.wait_ge(*q_link.at(I, RS * (t + 1)))
                pool.tensor_tensor(u[r][:].rearrange("p (h d) -> p h d", d=DH), u[r][:].rearrange("p (h d) -> p h d", d=DH),
                                   rn[:].unsqueeze(2).to_broadcast([P, 2 * H, DH]), ALU.mult).then_inc(*u_ready.up(I))

            def sq_(I, t):
                r = t % 2
                pool.wait_ge(*hi_ready.at(I, t + 1))
                pool.tensor_tensor(qst[r][:, :, DH:2 * DH], u[r][:, 0:INNER].rearrange("p (h d) -> p h d", h=H),
                                   qst[r][:, :, 0:DH], ALU.subtract).then_inc(*q_lo_ready.up(I))

            def h1(I, f):
                n = rows(f)
                pool.wait_ge(*hs_ready.at(I, f + 1))
                pool.tensor_tensor(hT_l[0:n, f, :], hp_[f % 2][0:n, :], hT_h[0:n, f, :], ALU.subtract).then_inc(*hl_ready.up(I))

            def l2(I, h):
                pool.wait_ge(*w.is_drained("L2", h))
                pool.tensor_tensor(mark_l[:, h:h + 1], mark_p[:], mark_p[:], ALU.add)
                own = Pl[h % 4][:].rearrange("p (j k) -> p j k", k=W)[:, 0:2 * NT - 1:2, :]
                nxt = Pl[h % 4][:].rearrange("p (j k) -> p j k", k=W)[:, 1:2 * NT - 1:2, :]
                pool.affine_select(out=own, in_=own, compare_op=ALU.is_ge, fill=0.0, base=0,
                                   pattern=[[0, NT], [1, W]], channel_multiplier=-1).then_inc(*masked.up(I))
                pool.affine_select(out=nxt, in_=nxt, compare_op=ALU.is_ge, fill=0.0, base=0,
                                   pattern=[[0, NT - 1], [-1, W]], channel_multiplier=1).then_inc(*masked.up(I))

            def ls(I):
                pool.wait_ge(*x1_ready.at(I, 1))
                pool.wait_ge(*y_stored.at(I, 0))
                pool.tensor_tensor(xb[:], x1[:], b2_t[:].unsqueeze(1).to_broadcast([P, NT, D]), ALU.add).then_inc(*xb_ready.up(I))

            with pool.Fori(0, L) as layer:
                w.run({"QK": qk, "SQ": sq_, "H1": h1, "L2": l2, "LS": ls}, layer)

        @block.sync
        def _(sp):
            hold = lambda at: stop(sp, at, sp_held)
            w = Walk(ph, sp, B)
            ph.start_credits(sp)

            def weights(I):
                K = layer_inst(w.layer)
                layer = w.layer
                done = Inst("layer_before", 0, None)
                done.b = layer * B
                hold(y_stored.at(done, 0))
                sp.wait_ge(const_done, N_CONST)
                def load(done, dst, src):
                    sp.dma_start(dst, src, allow_slow_non_contiguous=True).then_inc(*done.up(K, 16))
                load(wq_loaded, st_q, wqkv[layer].rearrange("(c p) n -> p c n", p=P))
                for c in range(NC):
                    load(w1_loaded, st_1[:, c, :], w1[layer][c * P:(c + 1) * P, :])
                load(w1_loaded, lnb[:], ln_b[layer].rearrange("(c p) -> p c", p=P))
                load(w1_loaded, lng[:], ln_g[layer].rearrange("(c p) -> p c", p=P))
                for g in range(2):
                    load(w1_loaded, b1_t[:, g, 0:NF - 1], b1[layer][g * HID:g * HID + (NF - 1) * P].rearrange("(f p) -> p f", p=P))
                    load(w1_loaded, b1_t[0:TAIL, g, NF - 1:NF],
                         b1[layer][g * HID + (NF - 1) * P:(g + 1) * HID].rearrange("(p o) -> p o", o=1))
                load(wo_loaded, st_o, wo[layer].rearrange("(c p) n -> p c n", p=P))
                load(wo_loaded, st_2[:, 0:NF - 1, :], w2[layer][0:(NF - 1) * P, :].rearrange("(f p) n -> p f n", p=P))
                load(wo_loaded, st_2[0:TAIL, NF - 1, :], w2[layer][(NF - 1) * P:HID, :])
                load(tables_loaded, cos_t[:], cos_d.rearrange("(t p) i d -> p t i d", p=P))
                load(tables_loaded, sin_t[:], sin_d.rearrange("(t p) i d -> p t i d", p=P))
                load(tables_loaded, qk_scale[:, 0, :], q_scale[layer].partition_broadcast(P))
                load(tables_loaded, qk_scale[:, 1, :], k_scale[layer].partition_broadcast(P))
                load(tables_loaded, b2_t[:], b2[layer].partition_broadcast(P))
                load(tables_loaded, is_last[:], last_only_d[layer].partition_broadcast(P))

            def xt(I):
                hold(xT_ready.before(I, 1))
                sp.dma_start(xs[:], out_v[I.local]).then_inc(*x_loaded.up(I, 16))

            def xr_(I):
                hold(x1_ready.before(I, 1))
                sp.dma_start(xr[:], out_v[I.local]).then_inc(*xr_loaded.up(I, 16))

            def lx(I):
                hold(x1_ready.at(I, 1))
                hold(xh_ready.before(I, 1))
                sp.dma_start(x1s[1:P, :, :], x1[0:P - 1, :, D // 2:D]).then_inc(*shifted.up(I, 16))
                sp.dma_start(x1s[0:1, 1:NT, :], x1[P - 1:P, 0:NT - 1, D // 2:D]).then_inc(*shifted.up(I, 16))
                hold(z_ready.before(I, 1))
                sp.dma_start(ar[:], res_v[I.local]).then_inc(*ar_loaded.up(I, 16))

            def w2_(I, part):
                if part < 2:
                    return
                hold(w.is_drained("W2"))
                sp.dma_start(out_v[I.local], xb[:]).then_inc(*y_stored.up(I, 16))

            with sp.Fori(0, L) as layer:
                w.run({"WB": weights, "XT": xt, "XR": xr_, "LX": lx, "W2": w2_}, layer)
            end = Inst("after", 0, None)
            end.b = L * B
            hold(y_stored.at(end, 0))

    return ph.measured()


def program(nc, counts, x, w_qkv, w_out, wqkv, q_scale, k_scale, wo, ln_g, ln_b, w1, b1, w2, b2, out):
    attn_res = nc.dram_tensor("attn_res", x.shape, F32, kind="Internal").ap()
    found = full_attention_phase(nc, counts, x, w_qkv, w_out, out, attn_res)
    return found | layers_phase(nc, counts, wqkv, q_scale, k_scale, wo, ln_g, ln_b, w1, b1, w2, b2, out, attn_res)


_INS = ["L0_attn_x", "L0_attn_w_qkv", "L0_attn_w_out", "L0_ffn_wqkv", "L0_ffn_q_scale", "L0_ffn_k_scale", "L0_ffn_wo",
        "L0_ffn_ln_g", "L0_ffn_ln_b", "L0_ffn_w1", "L0_ffn_b1", "L0_ffn_w2", "L0_ffn_b2"]
_TRANSPOSED = ("L0_attn_w_qkv", "L0_attn_w_out")


def kernel(**inputs):
    import concourse.bacc as bacc
    from concourse.bass_utils import run_bass_kernel_spmd

    arrays = {n: np.ascontiguousarray(inputs[n].T if n in _TRANSPOSED else inputs[n]) for n in _INS}

    def build(counts):
        nc = bacc.Bacc("TRN2", target_bir_lowering=False, num_devices=1)
        args = [nc.dram_tensor("in_" + n, arrays[n].shape, mybir.dt.from_np(arrays[n].dtype), kind="ExternalInput").ap()
                for n in _INS]
        out = nc.dram_tensor("out", arrays["L0_attn_x"].shape, F32, kind="ExternalOutput").ap()
        return nc, program(nc, counts, *args, out)

    _, counts = build({})
    nc, _ = build(counts)
    r = run_bass_kernel_spmd(nc, [{"in_" + n: arrays[n] for n in _INS}], core_ids=[0])
    return r.results[0]["out"]
```
